# Optimizing a Trainium2 kernel written in Bass

```python
import numpy as np
import jax
import jax.numpy as jnp

def _softmax(x, axis=-1):
    return jax.nn.softmax(x, axis=axis)

def _gelu(x):
    return jax.nn.gelu(x, approximate=True)

def _silu(x):
    return jax.nn.silu(x)

def _sigmoid(x):
    return jax.nn.sigmoid(x)

def _layernorm(x, axis=-1, eps=1e-05):
    m = jnp.mean(x, axis=axis, keepdims=True)
    v = jnp.var(x, axis=axis, keepdims=True)
    return (x - m) / jnp.sqrt(v + eps)

def _scatter_add(tgt, idx, src, axis=0):
    return tgt.at[idx].add(src)

def _segment_sum(src, seg, n):
    return jax.ops.segment_sum(src, seg, n)
kernel_name = 'mk_adj_resnorm_d4_adj_r2_d12529'

def setup_inputs(seed: int=0):
    np.random.seed(seed)
    _w = jnp.asarray

    def _rec_inputs():
        import jax
        import jax.numpy as jnp
        _gk = jax.random.key(seed)
        x = -0.0002928 + 1 * jax.random.normal(jax.random.fold_in(_gk, 1), (128, 128, 128), jnp.float32)
        _w = (1.0 + jnp.arange(128, dtype=jnp.float32)) ** (-0.5)
        _w = _w / _w.mean()
        _pij = jnp.clip(0.0625 * _w[:, None] * _w[None, :], 0.0, 1.0)
        _a = jax.random.uniform(jax.random.fold_in(_gk, 2), (128, 128, 128)) < _pij
        _a = jnp.logical_or(_a, jnp.eye(128, dtype=bool))
        _af = _a.astype(jnp.float32)
        _af = _af * jax.random.uniform(jax.random.fold_in(_gk, 3), (128, 128, 128), jnp.float32, 0.05, 1)
        adj = _af
        _nm = jnp.ones((128, 128), dtype=bool)
        nodemask = jnp.where(_nm, 1.0, 0.0).astype(jnp.int32)
        return (x, adj, nodemask)
    x, adj, nodemask = _rec_inputs()

    def _L0_gnn_setup():
        import jax, jax.numpy as jnp
        import numpy as np
        HIDDEN = 128
        NEG_INF = -1e+30
        key = jax.random.key(seed)
        k1, k2, k3, k4 = jax.random.split(key, 4)
        B, S, H = (4, 2048, HIDDEN)
        matrix = jax.random.normal(k1, (B, S, H), dtype=jnp.float32)
        mask = jax.random.randint(k2, (B, S), 0, 2, dtype=jnp.int32)
        adj = jax.random.uniform(k3, (B, S, S), dtype=jnp.float32)
        limit = float(np.sqrt(6.0 / (H + H)))
        W = jax.random.uniform(k4, (H, H), dtype=jnp.float32, minval=-limit, maxval=limit)
        return {'matrix': matrix, 'mask': mask, 'adj': adj, 'W': W}
    _L0_gnn_all = _L0_gnn_setup()
    _L0_gnn_in = {k: v for k, v in _L0_gnn_all.items() if k in ('W',)}
    del _L0_gnn_all

    def _L1_gnn_setup():
        import jax, jax.numpy as jnp
        import numpy as np
        key = jax.random.key(seed)
        k1, k2, k3, k4 = jax.random.split(key, 4)
        B, N, F_in, F_out = (8, 1024, 128, 128)
        x = jax.random.normal(k1, (B, N, F_in), dtype=jnp.float32)
        adj = jax.random.uniform(k2, (B, N, N), dtype=jnp.float32)
        stdv = 1.0 / np.sqrt(F_out)
        weight = jax.random.uniform(k3, (F_in, F_out), dtype=jnp.float32, minval=-stdv, maxval=stdv)
        bias = jax.random.uniform(k4, (F_out,), dtype=jnp.float32, minval=-stdv, maxval=stdv)
        return {'x': x, 'adj': adj, 'weight': weight, 'bias': bias}
    _L1_gnn_all = _L1_gnn_setup()
    _L1_gnn_in = {k: v for k, v in _L1_gnn_all.items() if k in ('weight', 'bias')}
    del _L1_gnn_all

    def _L2_gnn_setup():
        import jax, jax.numpy as jnp
        import numpy as np
        from jax import lax
        DIM = 128
        EPS = 1e-05

        def _bn(h, g, b, m, v):
            scale = g / jnp.sqrt(v + EPS)
            return h * scale[None, :, None] + (b - m * scale)[None, :, None]

        def _conv1d(h, w, pad):
            return lax.conv_general_dilated(h, w, window_strides=(1,), padding=[(pad, pad)], dimension_numbers=('NCH', 'OIH', 'NCH'))
        key = jax.random.key(seed)
        ks = jax.random.split(key, 16)
        bs, n, d = (16, 1024, DIM)
        s = 0.05
        return {'x': jax.random.normal(ks[0], (bs, n, d), jnp.float32), 'mask': jnp.ones((bs, n, n), jnp.float32), 'w_se': jax.random.normal(ks[1], (3, d), jnp.float32) * s, 'b_se': jnp.zeros((3,), jnp.float32), 'conv1_w': jax.random.normal(ks[2], (d, d, 1), jnp.float32) * s, 'bn1_g': jnp.ones((d,), jnp.float32), 'bn1_b': jnp.zeros((d,), jnp.float32), 'bn1_m': jnp.zeros((d,), jnp.float32), 'bn1_v': jnp.ones((d,), jnp.float32), 'conv2_w': jax.random.normal(ks[3], (d, d, 17), jnp.float32) * s, 'bn2_g': jnp.ones((d,), jnp.float32), 'bn2_b': jnp.zeros((d,), jnp.float32), 'bn2_m': jnp.zeros((d,), jnp.float32), 'bn2_v': jnp.ones((d,), jnp.float32), 'w_msg': jax.random.normal(ks[4], (d, d), jnp.float32) * s, 'b_msg': jnp.zeros((d,), jnp.float32), 'w_ih': jax.random.normal(ks[5], (3 * d, 2 * d), jnp.float32) * s, 'b_ih': jnp.zeros((3 * d,), jnp.float32), 'w_hh': jax.random.normal(ks[6], (3 * d, d), jnp.float32) * s, 'b_hh': jnp.zeros((3 * d,), jnp.float32)}
    _L2_gnn_all = _L2_gnn_setup()
    _L2_gnn_in = {k: v for k, v in _L2_gnn_all.items() if k in ('w_se', 'b_se', 'conv1_w', 'bn1_g', 'bn1_b', 'bn1_m', 'bn1_v', 'conv2_w', 'bn2_g', 'bn2_b', 'bn2_m', 'bn2_v', 'w_msg', 'b_msg', 'w_ih', 'b_ih', 'w_hh', 'b_hh')}
    del _L2_gnn_all

    def _L3_gnn_setup():
        import jax, jax.numpy as jnp
        import numpy as np
        B, N, F_IN, F_OUT = (8, 1024, 128, 128)
        key = jax.random.key(seed)
        k1, k2, k3, k4 = jax.random.split(key, 4)
        node_features = jax.random.normal(k1, (B, N, F_IN), dtype=jnp.float32)
        adj_matrix = jax.random.uniform(k2, (B, N, N), dtype=jnp.float32)
        lim = 1.0 / np.sqrt(F_IN)
        W = jax.random.uniform(k3, (F_OUT, F_IN), minval=-lim, maxval=lim, dtype=jnp.float32)
        b = jax.random.uniform(k4, (F_OUT,), minval=-lim, maxval=lim, dtype=jnp.float32)
        return {'node_features': node_features, 'adj_matrix': adj_matrix, 'W': W, 'b': b}
    _L3_gnn_all = _L3_gnn_setup()
    _L3_gnn_in = {k: v for k, v in _L3_gnn_all.items() if k in ('W', 'b')}
    del _L3_gnn_all
    return {'x': x, 'adj': adj, 'nodemask': nodemask, 'L0_gnn_W': _L0_gnn_in['W'], 'L1_gnn_weight': _L1_gnn_in['weight'], 'L1_gnn_bias': _L1_gnn_in['bias'], 'L2_gnn_w_se': _L2_gnn_in['w_se'], 'L2_gnn_b_se': _L2_gnn_in['b_se'], 'L2_gnn_conv1_w': _L2_gnn_in['conv1_w'], 'L2_gnn_bn1_g': _L2_gnn_in['bn1_g'], 'L2_gnn_bn1_b': _L2_gnn_in['bn1_b'], 'L2_gnn_bn1_m': _L2_gnn_in['bn1_m'], 'L2_gnn_bn1_v': _L2_gnn_in['bn1_v'], 'L2_gnn_conv2_w': _L2_gnn_in['conv2_w'], 'L2_gnn_bn2_g': _L2_gnn_in['bn2_g'], 'L2_gnn_bn2_b': _L2_gnn_in['bn2_b'], 'L2_gnn_bn2_m': _L2_gnn_in['bn2_m'], 'L2_gnn_bn2_v': _L2_gnn_in['bn2_v'], 'L2_gnn_w_msg': _L2_gnn_in['w_msg'], 'L2_gnn_b_msg': _L2_gnn_in['b_msg'], 'L2_gnn_w_ih': _L2_gnn_in['w_ih'], 'L2_gnn_b_ih': _L2_gnn_in['b_ih'], 'L2_gnn_w_hh': _L2_gnn_in['w_hh'], 'L2_gnn_b_hh': _L2_gnn_in['b_hh'], 'L3_gnn_W': _L3_gnn_in['W'], 'L3_gnn_b': _L3_gnn_in['b']}

def reference(x, adj, nodemask, L0_gnn_W, L1_gnn_weight, L1_gnn_bias, L2_gnn_w_se, L2_gnn_b_se, L2_gnn_conv1_w, L2_gnn_bn1_g, L2_gnn_bn1_b, L2_gnn_bn1_m, L2_gnn_bn1_v, L2_gnn_conv2_w, L2_gnn_bn2_g, L2_gnn_bn2_b, L2_gnn_bn2_m, L2_gnn_bn2_v, L2_gnn_w_msg, L2_gnn_b_msg, L2_gnn_w_ih, L2_gnn_b_ih, L2_gnn_w_hh, L2_gnn_b_hh, L3_gnn_W, L3_gnn_b):
    import jax
    import jax.numpy as jnp

    def _L0_gnn_ref(matrix, mask, adj, W):
        import jax, jax.numpy as jnp
        import numpy as np
        HIDDEN = 128
        NEG_INF = -1e+30
        intermediate = jnp.einsum('bsh,hd->bsd', matrix, W)
        similarities = jnp.einsum('bsd,btd->bst', intermediate, matrix)
        similarities = similarities * adj
        key_mask = mask[:, None, :].astype(bool)
        masked = jnp.where(key_mask, similarities, NEG_INF)
        attn = jax.nn.softmax(masked, axis=-1)
        output = jnp.einsum('bst,bth->bsh', attn, matrix)
        return output

    def _L1_gnn_ref(x, adj, weight, bias):
        import jax, jax.numpy as jnp
        import numpy as np
        support = jnp.einsum('bni,io->bno', x, weight)
        out = jnp.einsum('bnm,bmo->bno', adj, support)
        return out + bias

    def _L2_gnn_ref(x, mask, w_se, b_se, conv1_w, bn1_g, bn1_b, bn1_m, bn1_v, conv2_w, bn2_g, bn2_b, bn2_m, bn2_v, w_msg, b_msg, w_ih, b_ih, w_hh, b_hh):
        import jax, jax.numpy as jnp
        import numpy as np
        from jax import lax
        DIM = 128
        EPS = 1e-05

        def _bn(h, g, b, m, v):
            scale = g / jnp.sqrt(v + EPS)
            return h * scale[None, :, None] + (b - m * scale)[None, :, None]

        def _conv1d(h, w, pad):
            return lax.conv_general_dilated(h, w, window_strides=(1,), padding=[(pad, pad)], dimension_numbers=('NCH', 'OIH', 'NCH'))
        d = x.shape[-1]
        xc = jnp.transpose(x, (0, 2, 1))
        h = _bn(_conv1d(xc, conv1_w, 0), bn1_g, bn1_b, bn1_m, bn1_v)
        h = jax.nn.relu(h)
        h = _bn(_conv1d(h, conv2_w, 8), bn2_g, bn2_b, bn2_m, bn2_v)
        x_conv = jnp.transpose(jax.nn.relu(h + xc), (0, 2, 1))
        s = x @ w_se.T + b_se
        sq = jnp.sum(s * s, axis=-1)
        dist = sq[:, :, None] + sq[:, None, :] - 2.0 * jnp.einsum('bnd,bmd->bnm', s, s)
        A = jnp.exp(-dist) * mask
        msg = jax.nn.relu(x @ w_msg.T + b_msg)
        x_nmp = jnp.einsum('bnm,bmd->bnd', A, msg)
        x_in = jnp.concatenate([x_conv, x_nmp], axis=-1)
        gi = x_in @ w_ih.T + b_ih
        gh = x @ w_hh.T + b_hh
        gi_r, gi_z, gi_n = (gi[..., :d], gi[..., d:2 * d], gi[..., 2 * d:])
        gh_r, gh_z, gh_n = (gh[..., :d], gh[..., d:2 * d], gh[..., 2 * d:])
        r = jax.nn.sigmoid(gi_r + gh_r)
        z = jax.nn.sigmoid(gi_z + gh_z)
        nn_ = jnp.tanh(gi_n + r * gh_n)
        return (1.0 - z) * nn_ + z * x

    def _L3_gnn_ref(node_features, adj_matrix, W, b):
        import jax, jax.numpy as jnp
        import numpy as np
        B, N, F_IN, F_OUT = (8, 1024, 128, 128)
        degree = jnp.sum(adj_matrix, axis=-1)
        d_inv_sqrt = jnp.power(degree, -0.5)
        d_inv_sqrt = jnp.where(jnp.isinf(d_inv_sqrt), 0.0, d_inv_sqrt)
        norm_adj = adj_matrix * d_inv_sqrt[:, :, None] * d_inv_sqrt[:, None, :]
        transformed = jnp.einsum('bnf,of->bno', node_features, W) + b
        output = jnp.einsum('bnm,bmo->bno', norm_adj, transformed)
        return jax.nn.relu(output)
    x = _layernorm(x + _L0_gnn_ref(x, nodemask, adj, L0_gnn_W), axis=-1)
    x = _layernorm(x + _L1_gnn_ref(x, adj, L1_gnn_weight, L1_gnn_bias), axis=-1)
    x = _layernorm(x + _L2_gnn_ref(x, adj, L2_gnn_w_se, L2_gnn_b_se, L2_gnn_conv1_w, L2_gnn_bn1_g, L2_gnn_bn1_b, L2_gnn_bn1_m, L2_gnn_bn1_v, L2_gnn_conv2_w, L2_gnn_bn2_g, L2_gnn_bn2_b, L2_gnn_bn2_m, L2_gnn_bn2_v, L2_gnn_w_msg, L2_gnn_b_msg, L2_gnn_w_ih, L2_gnn_b_ih, L2_gnn_w_hh, L2_gnn_b_hh), axis=-1)
    x = _layernorm(x + _L3_gnn_ref(x, adj, L3_gnn_W, L3_gnn_b), axis=-1)
    return x

_drawn_inputs = setup_inputs


def setup_inputs(seed=0):
    import zlib

    import numpy as np

    out = dict(_drawn_inputs(seed))
    spreads = {'L2_gnn_b_se': (0.0, 0.8),
     'L2_gnn_bn1_g': (1.0, 0.6),
     'L2_gnn_bn1_b': (0.0, 0.451),
     'L2_gnn_bn1_m': (0.0, 0.406),
     'L2_gnn_bn1_v': (1.0, 0.6),
     'L2_gnn_bn2_g': (1.0, 0.2),
     'L2_gnn_bn2_b': (0.0, 0.688),
     'L2_gnn_bn2_m': (0.0, 0.68),
     'L2_gnn_bn2_v': (1.0, 0.6),
     'L2_gnn_b_msg': (0.0, 0.385),
     'L2_gnn_b_ih': (0.0, 0.1),
     'L2_gnn_b_hh': (0.0, 0.415)}
    factors = {}
    for name, (base, spread) in spreads.items():
        noise = np.random.default_rng([zlib.crc32(name.encode()), seed]).standard_normal(out[name].shape)
        drawn = base * np.exp(spread * noise) if base else spread * noise
        out[name] = jnp.asarray(drawn.astype(out[name].dtype))
    for name, factor in factors.items():
        out[name] = (out[name] * factor).astype(out[name].dtype)
    return out
```

```python
from contextlib import ExitStack

import concourse.bass as bass
from concourse import mybir

F32 = mybir.dt.float32
F32R = mybir.dt.float32r
I32 = mybir.dt.int32
ALU = mybir.AluOpType
ACT = mybir.ActivationFunctionType
AX = mybir.AxisListType

P = 128
Q = 4
W = Q * P
GROUPS = 128 // Q
TAPS = 17
PAD = TAPS // 2
PW = P + 2 * PAD
LAST_LAG = 3
FIRST_STEADY = 4
END_STEADY = GROUPS - 2
EPS = 1e-5
MASKED = 1e30
MAGIC = float(0x5F3759DF)
NEWTON = 3
LOADS = 5
NSTEP = 4 * NEWTON
VEC_STEPS = 2 + 3 * NEWTON + 7

U_W0, U_CONV1, U_CONV2 = 0, 1, 2
U_IH_CONV, U_IH_NMP, U_HH = U_CONV2 + TAPS, U_CONV2 + TAPS + 3, U_CONV2 + TAPS + 6
UNITS = U_HH + 3
GATE_R, GATE_Z, GATE_N = 0, 1, 2
SE = 3
VW = 32


def four_gnn_layers(nc, x_d, xT_d, adj_d, adjT_d, mask_d, w0_d, w1_d, b1_d, conv1_d, conv2_d,
                    bn_d, wih_d, whh_d, bih_d, bhh_d, wmsg_d, wse_d, bmsg_d, bse_d, w3_d, b3_d,
                    eye_d, out_d):
    ctx = ExitStack()
    with ctx:
        def sb(name, cols, dt=F32):
            return ctx.enter_context(nc.sbuf_tensor(name, [P, *cols], dt))

        def sem(name):
            return ctx.enter_context(nc.semaphore(name))

        adjT_all = sb("adjT_all", [GROUPS * W])
        staging = adjT_all[:, (GROUPS * W - UNITS * P):]
        w_hi = sb("w_hi", [UNITS * P], F32R)
        w_lo = sb("w_lo", [UNITS * P], F32R)
        w1 = sb("w1", [P])
        w3 = sb("w3", [P])
        w_msg = sb("w_msg", [P + SE])
        eye = sb("eye", [P])
        b1_row = sb("b1_row", [P])
        b3_row = sb("b3_row", [P])
        bmsg_row = sb("bmsg_row", [P])
        bse_row = sb("bse_row", [SE])
        bn = sb("bn", [8])
        bih = sb("bih", [3])
        bhh = sb("bhh", [3])
        aff = sb("aff", [4])
        gate_b = sb("gate_b", [4])
        tmp = sb("tmp", [8])
        dm_all = sb("dm_all", [GROUPS * Q])
        dm = sb("dm", [Q])

        x_in = [sb(f"x_in{p}", [W]) for p in range(2)]
        xT_in = [sb(f"xT_in{p}", [W]) for p in range(2)]
        adj_in = [sb(f"adj_in{p}", [W]) for p in range(2)]
        mask_in = [sb(f"mask_in{p}", [W], I32) for p in range(2)]
        xT_hi = sb("xT_hi", [W], F32R)
        xT_lo = sb("xT_lo", [W], F32R)
        mask_add = sb("mask_add", [W])
        deg = sb("deg", [Q])
        inter = sb("inter", [W])
        logit = sb("logit", [W])
        logit_min = sb("logit_min", [Q])
        prob = sb("prob", [W])
        prob_sum = sb("prob_sum", [Q])
        prob_inv = sb("prob_inv", [Q])
        probT = sb("probT", [W])
        res0 = sb("res0", [W])
        x1 = sb("x1", [W])
        aggT = sb("aggT", [W])
        x1_b = sb("x1_b", [W])
        res1 = sb("res1", [W])
        x2 = sb("x2", [W])
        x2T = [sb(f"x2T{p}", [W]) for p in range(2)]
        x2T_hi = sb("x2T_hi", [W], F32R)
        x2T_lo = sb("x2T_lo", [W], F32R)
        x2T_b = sb("x2T_b", [W])
        h1 = sb("h1", [W])
        h1_hi = sb("h1_hi", [Q, PW], F32R)
        h1_lo = sb("h1_lo", [Q, PW], F32R)
        msg_b = sb("msg_b", [W])
        msg = sb("msg", [W])
        vl = sb("vl", [Q, VW])
        vr = sb("vr", [Q * (P + VW)])
        s_sq = sb("s_sq", [Q, SE])
        s_sum_t = sb("s_sum_t", [Q])
        vlT = sb("vlT", [P])
        vrT = sb("vrT", [W])
        near = sb("near", [W])
        near_adjT = sb("near_adjT", [W])
        nmp_hi = sb("nmp_hi", [W], F32R)
        nmp_lo = sb("nmp_lo", [W], F32R)
        conv = sb("conv", [W])
        conv_hi = sb("conv_hi", [W], F32R)
        conv_lo = sb("conv_lo", [W], F32R)
        gr = sb("gr", [W])
        gz = sb("gz", [W])
        gh = sb("gh", [W])
        gw = sb("gw", [W])
        gn = sb("gn", [W])
        gd = sb("gd", [W])
        y = sb("y", [W])
        x3 = sb("x3", [W])
        x3T = sb("x3T", [W])
        lin3 = sb("lin3", [W])
        lin3_d = sb("lin3_d", [W])
        res3 = sb("res3", [W])
        x4 = sb("x4", [W])
        adjT3 = sb("adjT3", [W])
        stats = [sb(f"stats{i}", [Q, 6]) for i in range(4)]
        mv = [sb(f"mv{i}", [Q, 2]) for i in range(4)]
        var = [sb(f"var{i}", [2 * Q if i == 0 else Q]) for i in range(4)]
        rstd = [sb(f"rstd{i}", [2 * Q if i == 0 else Q]) for i in range(4)]
        nwt = [sb(f"nwt{i}", [2 * Q if i == 0 else Q]) for i in range(4)]
        neg_mean = [sb(f"neg_mean{i}", [Q]) for i in range(4)]
        shift = [sb(f"shift{i}", [Q]) for i in range(4)]

        def bank(name):
            return ctx.enter_context(nc.psum_tensor(name, [P, 512], F32))

        ps_a, ps_b, ps_c, ps_d = bank("ps_a"), bank("ps_b"), bank("ps_c"), bank("ps_d")
        ps_r, ps_z, ps_n, ps_h = bank("ps_r"), bank("ps_z"), bank("ps_n"), bank("ps_h")

        s_w = sem("s_w")
        s_whi, s_wlo = sem("s_whi"), sem("s_wlo")
        s_zero, s_const, s_vec = sem("s_zero"), sem("s_const"), sem("s_vec")
        s_load = [sem(f"s_load{p}") for p in range(2)]
        s_store, s_adj3 = sem("s_store"), sem("s_adj3")
        (s_xhi, s_xlo, s_mask, s_deg, s_interps, s_inter, s_scoreps, s_prod, s_logit, s_prob,
         s_probTps, s_probT, s_inv, s_out0ps, s_res0, s_x1, s_dm) = (sem(x) for x in (
            "s_xhi", "s_xlo", "s_mask", "s_deg", "s_interps", "s_inter", "s_scoreps", "s_prod",
            "s_logit", "s_prob", "s_probTps", "s_probT", "s_inv", "s_out0ps", "s_res0", "s_x1",
            "s_dm"))
        (s_aggps, s_agg, s_x1b, s_out1ps, s_res1, s_x2) = (sem(x) for x in (
            "s_aggps", "s_agg", "s_x1b", "s_out1ps", "s_res1", "s_x2"))
        (s_x2Tps, s_x2T, s_x2Thi, s_x2Tlo, s_x2Tb, s_conv1ps, s_h1, s_h1hi, s_h1lo, s_msgps, s_msgb,
         s_msg, s_emb, s_sq_sem, s_sum, s_v, s_vps, s_vlT, s_vrT, s_distps, s_near, s_nadj, s_nmpps,
         s_nmphi, s_nmplo, s_conv2ps, s_conv, s_convhi, s_convlo) = (sem(x) for x in (
            "s_x2Tps", "s_x2T", "s_x2Thi", "s_x2Tlo", "s_x2Tb", "s_conv1ps", "s_h1", "s_h1hi",
            "s_h1lo", "s_msgps", "s_msgb", "s_msg", "s_emb", "s_sq", "s_sum", "s_v", "s_vps",
            "s_vlT", "s_vrT", "s_distps", "s_near", "s_nadj", "s_nmpps", "s_nmphi", "s_nmplo",
            "s_conv2ps", "s_conv", "s_convhi", "s_convlo"))
        (s_ghps, s_gateps, s_gr, s_gh, s_gz, s_gw, s_gw2, s_gn, s_gd, s_ge, s_y) = (
            sem(x) for x in ("s_ghps", "s_gateps", "s_gr", "s_gh", "s_gz", "s_gw", "s_gw2",
                             "s_gn", "s_gd", "s_ge", "s_y"))
        (s_yTps, s_x3, s_x3Tps, s_x3T, s_lin3ps, s_lin3, s_dmc, s_lin3d, s_out3ps, s_relu3,
         s_res3, s_x4) = (sem(x) for x in (
            "s_yTps", "s_x3", "s_x3Tps", "s_x3T", "s_lin3ps", "s_lin3", "s_dmc", "s_lin3d",
            "s_out3ps", "s_relu3", "s_res3", "s_x4"))
        s_stats = [sem(f"s_stats{i}") for i in range(4)]
        s_mv = [sem(f"s_mv{i}") for i in range(4)]
        s_var = [sem(f"s_var{i}") for i in range(4)]
        s_guess = [sem(f"s_guess{i}") for i in range(4)]
        s_rstd = [sem(f"s_rstd{i}") for i in range(4)]
        s_shift = [sem(f"s_shift{i}") for i in range(4)]

        s_sq_, s_norm = s_sq_sem, sem("s_norm")

        def vr_of(a, b):
            return vr[:, :].rearrange("p (q c) -> p q c", q=Q)[:, :, a:b]

        def col(tile, q):
            return tile[:, q * P:(q + 1) * P]

        def quad(ap):
            return ap.rearrange("p (q n) -> p q n", q=Q)

        def row(tile, n=P):
            return tile[:, 0:n].unsqueeze(1).broadcast_to((P, Q, n))

        def per_graph(tile):
            return tile[:, 0:Q].unsqueeze(2).broadcast_to((P, Q, P))

        class Step:

            def __init__(self, eng, even, u, kept):
                self.eng, self.even, self.u, self.kept = eng, even, u, kept
                self.fixed = isinstance(even, int)
                self.p = u

            def has(self, lag):
                return not self.fixed or 0 <= self.even + self.u - lag < GROUPS

            def __call__(self, lag, k=1, less=0):
                c = self.u - lag + 1
                if self.fixed:
                    return k * min(self.even + c, GROUPS) - less
                if k not in self.kept:
                    self.kept[k] = {}
                if k == 1:
                    if c not in self.kept[k]:
                        self.kept[k][c] = self.eng.snap(self.even + c)
                    return self.kept[k][c]
                if 0 not in self.kept[k]:
                    self.kept[k][0] = self.eng.snap(self.even * k)
                return self.kept[k][0] + (k * c - less)

            def halves(self, lag, k):
                c = (self.u - lag) // 2 + 1
                if self.fixed:
                    return k * (self.even // 2 + c)
                if ("h", k) not in self.kept:
                    self.kept["h", k] = self.eng.snap(self.even * (k // 2))
                return self.kept["h", k] + k * c

            def at(self, lag, unit):
                return (self.even + (self.u - lag)) * unit

        def free(eng, sema, value):
            if not isinstance(value, int) or value > 0:
                eng.wait_ge(sema, value)

        def run(eng, step):
            for t in range(FIRST_STEADY):
                step(Step(eng, t - t % 2, t % 2, {}))
            with eng.Fori(FIRST_STEADY // 2, END_STEADY // 2) as pair:
                kept, even = {}, pair * 2
                for u in range(2):
                    step(Step(eng, even, u, kept))
            for t in range(END_STEADY, GROUPS + LAST_LAG):
                step(Step(eng, t - t % 2, t % 2, {}))

        block = ctx.enter_context(nc.Block())

        @block.sync
        def _(sp):
            def load(g, p):
                rows = bass.ds(g * P, P)
                sp.dma_start(xT_in[p][:, :], xT_d[rows, :]).then_inc(s_load[p], 16)
                sp.dma_start(adj_in[p][:, :], adj_d[rows, :]).then_inc(s_load[p], 16)
                sp.dma_start(mask_in[p][:, :], mask_d[bass.ds(g, 1), :].broadcast_to((P, W))).then_inc(s_load[p], 16)
                sp.dma_start(x_in[p][:, :], x_d[rows, :]).then_inc(s_load[p], 16)
                sp.dma_start(adjT_all[:, bass.ds(g * W, W)], adjT_d[rows, :]).then_inc(s_load[p], 16)

            load(0, 0)
            units = [(w0_d, U_W0, 1), (conv1_d, U_CONV1, 1), (conv2_d, U_CONV2, TAPS),
                     (wih_d[0:P, :], U_IH_CONV, 3), (wih_d[P:2 * P, :], U_IH_NMP, 3), (whh_d, U_HH, 3)]
            for src, u0, k in units:
                sp.dma_start(staging[:, u0 * P:(u0 + k) * P], src).then_inc(s_w, 16)
            for dst, src in [(w1[:, :], w1_d), (w3[:, :], w3_d), (w_msg[:, 0:P], wmsg_d),
                             (w_msg[:, P:P + SE], wse_d), (eye[:, :], eye_d),
                             (b1_row[:, :], b1_d.broadcast_to((P, P))),
                             (b3_row[:, :], b3_d.broadcast_to((P, P))),
                             (bmsg_row[:, :], bmsg_d.broadcast_to((P, P))),
                             (bse_row[:, :], bse_d.broadcast_to((P, SE))),
                             (bn[:, :], bn_d), (bih[:, :], bih_d), (bhh[:, :], bhh_d)]:
                sp.dma_start(dst, src).then_inc(s_const, 16)
            load(1, 1)

            def step(n):
                if n.has(0) and n.has(-2):
                    sp.wait_ge(s_res0, n(0))
                    load(n.even + (n.u + 2), n.p)
                if n.has(2):
                    free(sp, s_out3ps, n(3))
                    sp.dma_start(adjT3[:, :], adjT_all[:, bass.ds(n.at(2, W), W)]).then_inc(s_adj3, 16)
                if n.has(3):
                    sp.wait_ge(s_x4, n(3))
                    sp.dma_start(out_d[bass.ds(n.at(3, P), P), :], x4[:, :]).then_inc(s_store, 16)
            run(sp, step)
            sp.wait_ge(s_store, 16 * GROUPS)

        @block.tensor
        def _(pe):
            def split_product(ps, unit, hi, lo, start, stop):
                wh, wl = w_hi[:, unit * P:(unit + 1) * P], w_lo[:, unit * P:(unit + 1) * P]
                pe.matmul(ps, wh, hi, start=start, stop=False)
                pe.matmul(ps, wh, lo, start=False, stop=False)
                return pe.matmul(ps, wl, hi, start=False, stop=stop)

            def taps(a, b):
                for k in range(a, b):
                    mm = split_product(ps_n[:, :], U_CONV2 + k, h1_hi[:, :, k:k + P],
                                       h1_lo[:, :, k:k + P], k == 0, k == TAPS - 1)
                return mm

            pe.wait_ge(s_whi, 1)
            pe.wait_ge(s_wlo, 1)
            pe.wait_ge(s_const, 16 * 12)

            def step(n):
                if n.has(2):
                    pe.wait_ge(s_x2, n(2))
                    free(pe, s_nmphi, n(3))
                    free(pe, s_nmplo, n(3))
                    for q in range(Q):
                        mm = pe.transpose(col(ps_d, q), col(x2, q), eye[:, :])
                    mm.then_inc(s_x2Tps, 1)
                if n.has(1):
                    pe.wait_ge(s_x1, n(1))
                    for q in range(Q):
                        mm = pe.matmul(col(ps_a, q), col(x1, q),
                                       adjT_all[:, bass.ds(n.at(1, W) + q * P, P)], start=True, stop=True)
                    mm.then_inc(s_aggps, 1)
                if n.has(0):
                    pe.wait_ge(s_xhi, n(0))
                    pe.wait_ge(s_xlo, n(0))
                    free(pe, s_probT, n(1))
                    split_product(ps_b[:, :], U_W0, xT_hi[:, :], xT_lo[:, :], True, True).then_inc(s_interps, 1)
                if n.has(1):
                    pe.wait_ge(s_agg, n(1))
                    for q in range(Q):
                        mm = pe.matmul(col(ps_a, q), col(aggT, q), w1[:, :], start=True, stop=True)
                    mm.then_inc(s_out1ps, 1)
                if n.has(0):
                    pe.wait_ge(s_inter, n(0))
                    for q in range(Q):
                        mm = pe.matmul(col(ps_b, q), col(inter, q), col(xT_in[n.p], q), start=True, stop=True)
                    mm.then_inc(s_scoreps, 1)
                if n.has(2):
                    pe.wait_ge(s_x2Tb, n(2))
                    pe.wait_ge(s_x2Thi, n(2))
                    pe.wait_ge(s_x2Tlo, n(2))
                    split_product(ps_d[:, :], U_CONV1, x2T_hi[:, :], x2T_lo[:, :], True, True).then_inc(s_conv1ps, 1)
                    free(pe, s_gr, n(3))
                    free(pe, s_gz, n(3))
                    for q in range(Q):
                        dst = (ps_r if q < 2 else ps_z)[:, (q % 2) * (P + SE):(q % 2 + 1) * (P + SE)]
                        mm = pe.matmul(dst, col(x2T[n.p], q), w_msg[:, :], start=True, stop=True)
                    mm.then_inc(s_msgps, 1)
                    pe.wait_ge(s_h1hi, n(2))
                    pe.wait_ge(s_h1lo, n(2))
                    free(pe, s_gw2, n(3))
                    taps(0, 4)
                if n.has(3):
                    pe.wait_ge(s_y, n(3))
                    free(pe, s_relu3, n(4))
                    for q in range(Q):
                        mm = pe.transpose(col(ps_c, q), col(y, q), eye[:, :])
                    mm.then_inc(s_yTps, 1)
                if n.has(2):
                    pe.wait_ge(s_v, n(2))
                    pe.wait_ge(s_h1, n(2))
                    free(pe, s_gh, n(3))
                    pe.transpose(ps_d[:, 0:P], vl[:, :, :].rearrange("p q c -> p (q c)"), eye[:, :])
                    for q in range(Q):
                        mm = pe.transpose(col(ps_h, q), vr[:, q * P:(q + 1) * P], eye[:, :])
                    mm.then_inc(s_vps, 1)
                if n.has(0):
                    pe.wait_ge(s_prob, n(0))
                    for q in range(Q):
                        mm = pe.transpose(col(ps_b, q), col(prob, q), eye[:, :])
                    mm.then_inc(s_probTps, 1)
                if n.has(2):
                    taps(4, 7)
                    pe.wait_ge(s_vlT, n(2))
                    pe.wait_ge(s_vrT, n(2))
                    pe.matmul(ps_d[:, :], vlT[:, :], vrT[:, :], start=True, stop=True).then_inc(s_distps, 1)
                if n.has(0):
                    pe.wait_ge(s_probT, n(0))
                    free(pe, s_res1, n(1))
                    for q in range(Q):
                        mm = pe.matmul(col(ps_a, q), col(probT, q), col(x_in[n.p], q), start=True, stop=True)
                    mm.then_inc(s_out0ps, 1)
                if n.has(2):
                    taps(7, 11)
                if n.has(3):
                    pe.wait_ge(s_x3, n(3))
                    for q in range(Q):
                        mm = pe.transpose(col(ps_c, q), col(x3, q), eye[:, :])
                    mm.then_inc(s_x3Tps, 1)
                if n.has(2):
                    pe.wait_ge(s_nadj, n(2))
                    pe.wait_ge(s_msg, n(2))
                    for q in range(Q):
                        mm = pe.matmul(col(ps_d, q), col(msg, q), col(near_adjT, q), start=True, stop=True)
                    mm.then_inc(s_nmpps, 1)
                    taps(11, 13)
                if n.has(3):
                    pe.wait_ge(s_x3T, n(3))
                    for q in range(Q):
                        mm = pe.matmul(col(ps_c, q), col(x3T, q), w3[:, :], start=True, stop=True)
                    mm.then_inc(s_lin3ps, 1)
                if n.has(2):
                    taps(13, TAPS).then_inc(s_conv2ps, 1)
                if n.has(3):
                    pe.wait_ge(s_lin3d, n(3))
                    pe.wait_ge(s_adj3, n(3, 16))
                    for q in range(Q):
                        mm = pe.matmul(col(ps_c, q), col(adjT3, q), col(lin3_d, q), start=True, stop=True)
                    mm.then_inc(s_out3ps, 1)
                if n.has(2):
                    pe.wait_ge(s_nmphi, n(2))
                    pe.wait_ge(s_nmplo, n(2))
                    pe.wait_ge(s_msg, n(2))
                    for ps, gate in ((ps_r, GATE_R), (ps_z, GATE_Z)):
                        split_product(ps[:, :], U_HH + gate, x2T_hi[:, :], x2T_lo[:, :], True, False)
                        split_product(ps[:, :], U_IH_NMP + gate, nmp_hi[:, :], nmp_lo[:, :], False, False)
                    split_product(ps_h[:, :], U_HH + GATE_N, x2T_hi[:, :], x2T_lo[:, :], True, True).then_inc(s_ghps, 1)
                    pe.wait_ge(s_convhi, n(2))
                    pe.wait_ge(s_convlo, n(2))
                    split_product(ps_r[:, :], U_IH_CONV + GATE_R, conv_hi[:, :], conv_lo[:, :], False, True).then_inc(s_gateps, 1)
                    split_product(ps_n[:, :], U_IH_NMP + GATE_N, nmp_hi[:, :], nmp_lo[:, :], True, False)
                    split_product(ps_n[:, :], U_IH_CONV + GATE_N, conv_hi[:, :], conv_lo[:, :], False, True).then_inc(s_gateps, 1)
                    split_product(ps_z[:, :], U_IH_CONV + GATE_Z, conv_hi[:, :], conv_lo[:, :], False, True).then_inc(s_gateps, 1)
            run(pe, step)

        @block.scalar
        def _(act):
            act.wait_ge(s_w, 16 * 6)
            act.copy(w_hi[:, :], staging).then_inc(s_whi, 1)

            def split_x(n):
                act.wait_ge(s_load[1 - n.p], n.halves(-1, 16 * LOADS))
                free(act, s_interps, n(0))
                act.copy(xT_hi[:, :], xT_in[1 - n.p][:, :]).then_inc(s_xhi, 1)

            def apply(i, out, src, n, lag, done):
                act.wait_ge(s_shift[i], n(lag))
                for q in range(Q):
                    ins = act.activation(col(out, q), col(src, q), ACT.Identity, bias=shift[i][:, q:q + 1],
                                         scale=rstd[i][:, q:q + 1])
                ins.then_inc(done, 1)

            act.wait_ge(s_load[0], 16 * LOADS)
            act.copy(xT_hi[:, :], xT_in[0][:, :]).then_inc(s_xhi, 1)
            act.wait_ge(s_vec, VEC_STEPS)

            def step(n):
                if n.has(2):
                    act.wait_ge(s_x2Tps, n(2))
                    free(act, s_y, n(4))
                    act.copy(x2T[n.p][:, :], ps_d[:, :]).then_inc(s_x2T, 1)
                    free(act, s_ghps, n(3))
                    act.copy(x2T_hi[:, :], ps_d[:, :]).then_inc(s_x2Thi, 1)
                    free(act, s_conv, n(3))
                    act.activation(x2T_b[:, :], ps_d[:, :], ACT.Identity, bias=aff[:, 3:4]).then_inc(s_x2Tb, 1)
                if n.has(3):
                    act.wait_ge(s_gateps, n(3, 3, 2))
                    free(act, s_gw, n(4))
                    act.activation(gr[:, :], ps_r[:, :], ACT.Tanh, bias=gate_b[:, 0:1], scale=0.5).then_inc(s_gr, 1)
                    act.activation(gh[:, :], ps_h[:, :], ACT.Identity, bias=gate_b[:, 2:3], scale=0.5).then_inc(s_gh, 1)
                if n.has(1):
                    act.wait_ge(s_aggps, n(1))
                    free(act, s_out1ps, n(2))
                    act.copy(aggT[:, :], ps_a[:, :]).then_inc(s_agg, 1)
                if n.has(0):
                    act.wait_ge(s_interps, n(0))
                    free(act, s_scoreps, n(1))
                    act.mul(inter[:, :], ps_b[:, :], -1.0).then_inc(s_inter, 1)
                if n.has(3):
                    act.wait_ge(s_gateps, n(3, 3))
                    free(act, s_ge, n(4))
                    act.activation(gz[:, :], ps_z[:, :], ACT.Tanh, bias=gate_b[:, 1:2], scale=0.5).then_inc(s_gz, 1)
                    act.wait_ge(s_gw2, n(3))
                    free(act, s_gd, n(4))
                    act.activation(gn[:, :], gw[:, :], ACT.Tanh, bias=gate_b[:, 3:4]).then_inc(s_gn, 1)
                if n.has(2):
                    act.wait_ge(s_conv1ps, n(2))
                    free(act, s_h1lo, n(3))
                    act.activation(h1[:, :], ps_d[:, :], ACT.Relu, bias=aff[:, 2:3], scale=aff[:, 0:1]).then_inc(s_h1, 1)
                    act.wait_ge(s_h1, n(2))
                    free(act, s_conv2ps, n(3))
                    act.copy(h1_hi[:, :, PAD:PAD + P], quad(h1[:, :])).then_inc(s_h1hi, 1)
                    act.wait_ge(s_msgb, n(2))
                    free(act, s_nmpps, n(3))
                    act.activation(msg[:, :], msg_b[:, :], ACT.Relu).then_inc(s_msg, 1)
                if n.has(0):
                    act.wait_ge(s_logit, n(0))
                    free(act, s_probTps, n(1))
                    free(act, s_inv, n(1))
                    for q in range(Q):
                        ins = act.activation(col(prob, q), col(logit, q), ACT.Exp, bias=logit_min[:, q:q + 1],
                                             scale=-1.0, accum_out=prob_sum[:, q:q + 1])
                    ins.then_inc(s_prob, 1)
                if n.has(2):
                    act.wait_ge(s_vps, n(2))
                    free(act, s_distps, n(3))
                    act.copy(vlT[:, :], ps_d[:, 0:P]).then_inc(s_vlT, 1)
                    act.copy(vrT[:, :], ps_h[:, :]).then_inc(s_vrT, 1)
                if n.has(0):
                    act.wait_ge(s_probTps, n(0))
                    free(act, s_out0ps, n(1))
                    act.copy(probT[:, :], ps_b[:, :]).then_inc(s_probT, 1)
                if n.has(2):
                    act.wait_ge(s_distps, n(2))
                    free(act, s_nadj, n(3))
                    act.activation(near[:, :], ps_d[:, :], ACT.Exp).then_inc(s_near, 1)
                if n.has(1):
                    free(act, s_x2Tps, n(2))
                    apply(1, x2, res1, n, 1, s_x2)
                if n.has(3):
                    free(act, s_res3, n(4))
                    apply(2, x3, ps_c, n, 3, s_x3)
                    act.wait_ge(s_x3Tps, n(3))
                    free(act, s_lin3ps, n(4))
                    act.copy(x3T[:, :], ps_c[:, :]).then_inc(s_x3T, 1)
                if n.has(2):
                    act.wait_ge(s_nmpps, n(2))
                    free(act, s_gateps, n(3, 3))
                    act.copy(nmp_hi[:, :], ps_d[:, :]).then_inc(s_nmphi, 1)
                if n.has(0):
                    free(act, s_aggps, n(1))
                    free(act, s_x1b, n(1))
                    apply(0, x1, res0, n, 0, s_x1)
                if n.has(-1):
                    split_x(n)
                if n.has(2):
                    act.wait_ge(s_conv, n(2))
                    act.activation(conv_hi[:, :], conv[:, :], ACT.Relu).then_inc(s_convhi, 1)
            run(act, step)

        @block.vector
        def _(dve):
            def held():
                dve.nop(nofuse=True)

            for tile in (h1_hi, h1_lo):
                dve.memset(tile[:, :, :].bitcast(F32), 0.0).then_inc(s_zero, 1)
            dve.memset(vl[:, :, :], 0.0).then_inc(s_zero, 1)
            dve.memset(vr[:, :], 0.0).then_inc(s_zero, 1)
            dve.wait_ge(s_zero, 4)
            dve.memset(vl[:, :, 4:5], 1.0).then_inc(s_zero, 1)
            dve.memset(vr_of(3, 4), -1.0).then_inc(s_zero, 1)

            vec = [0]

            def chain(ins):
                ins.then_inc(s_vec, 1)
                vec[0] += 1
                dve.wait_ge(s_vec, vec[0])

            two = lambda tile, a: tile[:, a:a + 5:4]
            dve.wait_ge(s_const, 16 * 12)
            v, g, a = tmp[:, 0:2], tmp[:, 2:4], tmp[:, 4:6]
            chain(dve.tensor_scalar(v, two(bn, 3), EPS, None, ALU.add))
            chain(dve.tensor_scalar(g.bitcast(I32), v.bitcast(I32), -0.5, MAGIC, ALU.mult, ALU.add))
            for _ in range(NEWTON):
                chain(dve.scalar_tensor_tensor(out=a, in0=g, scalar=-0.5, in1=g, op0=ALU.mult, op1=ALU.mult))
                chain(dve.tensor_tensor(a, a, v, ALU.mult))
                chain(dve.scalar_tensor_tensor(out=g, in0=a, scalar=1.5, in1=g, op0=ALU.add, op1=ALU.mult))
            chain(dve.tensor_tensor(aff[:, 0:2], two(bn, 0), g, ALU.mult))
            chain(dve.tensor_tensor(a, two(bn, 2), aff[:, 0:2], ALU.mult))
            chain(dve.tensor_tensor(aff[:, 2:4], two(bn, 1), a, ALU.subtract))
            chain(dve.tensor_tensor(a, bih[:, 0:2], bhh[:, 0:2], ALU.add))
            chain(dve.tensor_scalar(gate_b[:, 0:2], a, 0.5, None, ALU.mult))
            chain(dve.tensor_scalar(gate_b[:, 2:3], bhh[:, 2:3], 0.5, None, ALU.mult))
            chain(dve.tensor_copy(gate_b[:, 3:4], bih[:, 2:3]))
            assert vec[0] == VEC_STEPS

            dve.wait_ge(s_whi, 1)
            dve.tensor_tensor(w_lo[:, :], staging, w_hi[:, :].bitcast(F32), ALU.subtract).then_inc(s_wlo, 1)

            def look(i, src, n, lag):
                for q in range(Q):
                    ins = dve.bn_stats(stats[i][:, q, :], col(src, q))
                ins.then_inc(s_stats[i], 1)

            def moments(i, n, lag):
                dve.wait_ge(s_stats[i], n(lag))
                held()
                for q in range(Q):
                    ins = dve.bn_aggr(mv[i][:, q, :], stats[i][:, q, :])
                ins.then_inc(s_mv[i], 1)

            def spread(i, n, lag):
                dve.wait_ge(s_mv[i], n(lag))
                eps = 4 * EPS if i == 2 else EPS
                dve.tensor_scalar(neg_mean[i][:, :], mv[i][:, :, 0], -1.0, None, ALU.mult)
                dve.tensor_scalar(var[i][:, 0:Q], mv[i][:, :, 1], eps, None, ALU.add).then_inc(s_var[i], 1)

            def guess(i, n, lag):
                dve.wait_ge(s_var[i], n(lag))
                dve.tensor_scalar(rstd[i][:, :].bitcast(I32), var[i][:, :].bitcast(I32), -0.5, MAGIC,
                                  ALU.mult, ALU.add).then_inc(s_guess[i], 1)

            def apply(i, out, src, n, lag, done):
                dve.wait_ge(s_rstd[i], n(lag, NSTEP))
                for q in range(Q):
                    ins = dve.tensor_scalar(col(out, q), col(src, q), mv[i][:, q, 0:1], rstd[i][:, q:q + 1],
                                            ALU.subtract, ALU.mult)
                ins.then_inc(done, 1)

            def prepare(n, lag):
                p = (n.p + lag) % 2
                dve.wait_ge(s_load[p], n.halves(lag, 16 * LOADS))
                free(dve, s_logit, n(lag + 1))
                dve.tensor_scalar(mask_add[:, :], mask_in[p][:, :], 0, MASKED, ALU.is_equal, ALU.mult).then_inc(s_mask, 1)
                free(dve, s_dm, n(lag + 1))
                dve.tensor_reduce(deg[:, :], quad(adj_in[p][:, :]), AX.X, ALU.add).then_inc(s_deg, 1)

            dve.wait_ge(s_load[0], 16 * LOADS)
            dve.tensor_scalar(mask_add[:, :], mask_in[0][:, :], 0, MASKED, ALU.is_equal, ALU.mult).then_inc(s_mask, 1)
            dve.tensor_reduce(deg[:, :], quad(adj_in[0][:, :]), AX.X, ALU.add).then_inc(s_deg, 1)

            def step(n):
                if n.has(2):
                    dve.wait_ge(s_x2Thi, n(2))
                    free(dve, s_ghps, n(3))
                    dve.tensor_tensor(x2T_lo[:, :], x2T[n.p][:, :], x2T_hi[:, :].bitcast(F32), ALU.subtract).then_inc(s_x2Tlo, 1)
                if n.has(1):
                    dve.wait_ge(s_out1ps, n(1))
                    dve.wait_ge(s_x1b, n(1))
                    free(dve, s_x2, n(2))
                    dve.tensor_tensor(res1[:, :], ps_a[:, :], x1_b[:, :], ALU.add).then_inc(s_res1, 1)
                if n.has(3):
                    dve.wait_ge(s_gr, n(3))
                    dve.wait_ge(s_gh, n(3))
                    free(dve, s_gn, n(4))
                    dve.scalar_tensor_tensor(out=gw[:, :], in0=gr[:, :], scalar=1.0, in1=gh[:, :],
                                             op0=ALU.add, op1=ALU.mult).then_inc(s_gw, 1)
                if n.has(0):
                    dve.wait_ge(s_scoreps, n(0))
                    free(dve, s_prob, n(1))
                    dve.tensor_tensor(logit[:, :], ps_b[:, :], adj_in[n.p][:, :], ALU.mult).then_inc(s_prod, 1)
                if n.has(1):
                    dve.wait_ge(s_res1, n(1))
                    look(1, res1, n, 1)
                if n.has(3):
                    dve.wait_ge(s_gw, n(3))
                    dve.wait_ge(s_gateps, n(3, 3, 1))
                    dve.tensor_tensor(gw[:, :], gw[:, :], ps_n[:, :], ALU.add).then_inc(s_gw2, 1)
                if n.has(0):
                    dve.wait_ge(s_prod, n(0))
                    dve.wait_ge(s_mask, n(0))
                    held()
                    for q in range(Q):
                        ins = dve.tensor_tensor_reduce(col(logit, q), col(logit, q), col(mask_add, q), 1.0, MASKED * 2,
                                                       ALU.add, ALU.min, logit_min[:, q:q + 1])
                    ins.then_inc(s_logit, 1)
                if n.has(1):
                    moments(1, n, 1)
                if n.has(2):
                    dve.wait_ge(s_msgps, n(2))
                    free(dve, s_vps, n(3))
                    for h in range(2):
                        part = (ps_r, ps_z)[h][:, 0:2 * (P + SE)].rearrange("p (q c) -> p q c", q=2)
                        ins = dve.tensor_tensor(vl[:, 2 * h:2 * h + 2, 0:SE], part[:, :, P:P + SE],
                                                bse_row[:, :].unsqueeze(1).broadcast_to((P, 2, SE)), ALU.add)
                    ins.then_inc(s_emb, 1)
                if n.has(1):
                    spread(1, n, 1)
                if n.has(2):
                    free(dve, s_msg, n(3))
                    for h in range(2):
                        part = (ps_r, ps_z)[h][:, 0:2 * (P + SE)].rearrange("p (q c) -> p q c", q=2)
                        ins = dve.tensor_tensor(quad(msg_b[:, :])[:, 2 * h:2 * h + 2, :], part[:, :, 0:P],
                                                bmsg_row[:, :].unsqueeze(1).broadcast_to((P, 2, P)), ALU.add)
                    ins.then_inc(s_msgb, 1)
                if n.has(3):
                    dve.wait_ge(s_gd, n(3))
                    dve.wait_ge(s_gz, n(3))
                    dve.scalar_tensor_tensor(out=gd[:, :], in0=gz[:, :], scalar=-1.0, in1=gd[:, :],
                                             op0=ALU.add, op1=ALU.mult).then_inc(s_ge, 1)
                if n.has(1):
                    guess(1, n, 1)
                if n.has(3):
                    dve.wait_ge(s_ge, n(3))
                    free(dve, s_yTps, n(4))
                    dve.scalar_tensor_tensor(out=y[:, :], in0=x2T[1 - n.p][:, :], scalar=4.0, in1=gd[:, :],
                                             op0=ALU.mult, op1=ALU.add).then_inc(s_y, 1)
                if n.has(0):
                    dve.wait_ge(s_prob, n(0))
                    dve.reciprocal(prob_inv[:, :], prob_sum[:, :]).then_inc(s_inv, 1)
                if n.has(3):
                    dve.wait_ge(s_yTps, n(3))
                    held()
                    look(2, ps_c, n, 3)
                if n.has(0):
                    dve.wait_ge(s_out0ps, n(0))
                    dve.wait_ge(s_inv, n(0))
                    free(dve, s_x1, n(1))
                    for q in range(Q):
                        ins = dve.scalar_tensor_tensor(out=col(res0, q), in0=col(ps_a, q), scalar=prob_inv[:, q:q + 1],
                                                       in1=col(x_in[n.p], q), op0=ALU.mult, op1=ALU.add)
                    ins.then_inc(s_res0, 1)
                if n.has(3):
                    moments(2, n, 3)
                if n.has(2):
                    dve.wait_ge(s_near, n(2))
                    free(dve, s_nmpps, n(3))
                    dve.tensor_tensor(near_adjT[:, :], near[:, :], adjT_all[:, bass.ds(n.at(2, W), W)], ALU.mult).then_inc(s_nadj, 1)
                if n.has(3):
                    spread(2, n, 3)
                if n.has(0):
                    dve.wait_ge(s_res0, n(0))
                    look(0, res0, n, 0)
                if n.has(3):
                    guess(2, n, 3)
                if n.has(0):
                    dve.wait_ge(s_deg, n(0))
                    dve.scalar_tensor_tensor(out=var[0][:, Q:2 * Q], in0=deg[:, :], scalar=0.0, in1=deg[:, :],
                                             op0=ALU.is_equal, op1=ALU.add)
                    moments(0, n, 0)
                if n.has(2):
                    dve.wait_ge(s_nmphi, n(2))
                    free(dve, s_gateps, n(3, 3))
                    dve.tensor_tensor(nmp_lo[:, :], ps_d[:, :], nmp_hi[:, :].bitcast(F32), ALU.subtract).then_inc(s_nmplo, 1)
                if n.has(0):
                    spread(0, n, 0)
                if n.has(3):
                    dve.wait_ge(s_lin3ps, n(3))
                    free(dve, s_lin3d, n(4))
                    free(dve, s_relu3, n(4))
                    dve.tensor_tensor(quad(lin3[:, :]), quad(ps_c[:, :]), row(b3_row), ALU.add).then_inc(s_lin3, 1)
                    dve.tensor_copy(dm[:, :], dm_all[:, bass.ds(n.at(3, Q), Q)]).then_inc(s_dmc, 1)
                if n.has(0):
                    guess(0, n, 0)
                if n.has(3):
                    dve.wait_ge(s_out3ps, n(3))
                    dve.wait_ge(s_dmc, n(3))
                    free(dve, s_x4, n(4))
                    dve.scalar_tensor_tensor(out=quad(res3[:, :]), in0=quad(ps_c[:, :]), scalar=0.0, in1=per_graph(dm),
                                             op0=ALU.max, op1=ALU.mult).then_inc(s_relu3, 1)
                if n.has(0):
                    dve.wait_ge(s_rstd[0], n(0, NSTEP))
                    dve.scalar_tensor_tensor(out=dm_all[:, bass.ds(n.at(0, Q), Q)], in0=deg[:, :], scalar=0.0,
                                             in1=rstd[0][:, Q:2 * Q], op0=ALU.not_equal, op1=ALU.mult).then_inc(s_dm, 1)
                if n.has(2):
                    dve.wait_ge(s_conv2ps, n(2))
                    dve.wait_ge(s_x2Tb, n(2))
                    free(dve, s_convhi, n(3))
                    free(dve, s_convlo, n(3))
                    dve.scalar_tensor_tensor(out=conv[:, :], in0=ps_n[:, :], scalar=aff[:, 1:2], in1=x2T_b[:, :],
                                             op0=ALU.mult, op1=ALU.add).then_inc(s_conv, 1)
                if n.has(3):
                    dve.wait_ge(s_res3, n(3))
                    look(3, res3, n, 3)
                    moments(3, n, 3)
                    spread(3, n, 3)
                    guess(3, n, 3)
                if n.has(-1):
                    prepare(n, -1)
                if n.has(2):
                    dve.wait_ge(s_convhi, n(2))
                    free(dve, s_gateps, n(3, 3))
                    dve.scalar_tensor_tensor(out=conv_lo[:, :], in0=conv[:, :], scalar=0.0, in1=conv_hi[:, :].bitcast(F32),
                                             op0=ALU.max, op1=ALU.subtract).then_inc(s_convlo, 1)
                if n.has(3):
                    free(dve, s_store, n(4, 16))
                    apply(3, x4, res3, n, 3, s_x4)
            run(dve, step)

        @block.gpsimd
        def _(pool):
            def held():
                pool.nop(nofuse=True)

            def newton(i, n, lag):
                v, y_, a = var[i][:, :], rstd[i][:, :], nwt[i][:, :]
                pool.wait_ge(s_guess[i], n(lag))
                for k in range(NEWTON):
                    left = NSTEP - 4 * k
                    if k:
                        pool.wait_ge(s_rstd[i], n(lag, NSTEP, left))
                    pool.tensor_tensor(a, y_, y_, ALU.mult).then_inc(s_rstd[i], 1)
                    pool.wait_ge(s_rstd[i], n(lag, NSTEP, left - 1))
                    pool.tensor_tensor(a, a, v, ALU.mult).then_inc(s_rstd[i], 1)
                    pool.wait_ge(s_rstd[i], n(lag, NSTEP, left - 2))
                    held()
                    pool.tensor_scalar(a, a, -0.5, 1.5, ALU.mult, ALU.add).then_inc(s_rstd[i], 1)
                    pool.wait_ge(s_rstd[i], n(lag, NSTEP, left - 3))
                    pool.tensor_tensor(y_, a, y_, ALU.mult).then_inc(s_rstd[i], 1)

            def shifts(i, n, lag):
                pool.wait_ge(s_rstd[i], n(lag, NSTEP))
                pool.tensor_tensor(shift[i][:, :], neg_mean[i][:, :], rstd[i][:, 0:Q], ALU.mult).then_inc(s_shift[i], 1)

            pool.wait_ge(s_xhi, 1)
            pool.tensor_tensor(xT_lo[:, :], xT_in[0][:, :], xT_hi[:, :].bitcast(F32), ALU.subtract).then_inc(s_xlo, 1)
            pool.wait_ge(s_zero, 6)

            def step(n):
                if n.has(2):
                    pool.wait_ge(s_h1hi, n(2))
                    free(pool, s_conv2ps, n(3))
                    pool.tensor_tensor(h1_lo[:, :, PAD:PAD + P], quad(h1[:, :]), h1_hi[:, :, PAD:PAD + P].bitcast(F32),
                                       ALU.subtract).then_inc(s_h1lo, 1)
                if n.has(3):
                    pool.wait_ge(s_gn, n(3))
                    free(pool, s_y, n(4))
                    pool.tensor_tensor(gd[:, :], x2T[1 - n.p][:, :], gn[:, :], ALU.subtract).then_inc(s_gd, 1)
                if n.has(1):
                    newton(1, n, 1)
                    free(pool, s_x2, n(2))
                    shifts(1, n, 1)
                if n.has(2):
                    e = vl[:, :, 0:SE]
                    pool.wait_ge(s_emb, n(2))
                    pool.tensor_tensor(s_sq[:, :, :], e, e, ALU.mult).then_inc(s_sq_, 1)
                    pool.tensor_tensor(vr_of(0, SE), e, e, ALU.add)
                    pool.wait_ge(s_sq_, n(2))
                    pool.tensor_tensor(s_sum_t[:, :], s_sq[:, :, 0], s_sq[:, :, 1], ALU.add).then_inc(s_sum, 1)
                    pool.wait_ge(s_sum, n(2))
                    pool.tensor_tensor(vl[:, :, 3], s_sum_t[:, :], s_sq[:, :, 2], ALU.add).then_inc(s_norm, 1)
                    pool.wait_ge(s_norm, n(2))
                    held()
                    pool.tensor_scalar(vr_of(4, 5), vl[:, :, 3:4], -1.0, None, ALU.mult).then_inc(s_v, 1)
                if n.has(3):
                    newton(2, n, 3)
                    free(pool, s_x3, n(4))
                    shifts(2, n, 3)
                if n.has(0):
                    newton(0, n, 0)
                    free(pool, s_x1, n(1))
                    shifts(0, n, 0)
                if n.has(3):
                    pool.wait_ge(s_lin3, n(3))
                    pool.wait_ge(s_dmc, n(3))
                    free(pool, s_out3ps, n(4))
                    pool.tensor_tensor(quad(lin3_d[:, :]), quad(lin3[:, :]), per_graph(dm), ALU.mult).then_inc(s_lin3d, 1)
                    pool.wait_ge(s_relu3, n(3))
                    pool.wait_ge(s_x3, n(3))
                    pool.tensor_tensor(res3[:, :], res3[:, :], x3[:, :], ALU.add).then_inc(s_res3, 1)
                if n.has(0):
                    pool.wait_ge(s_x1, n(0))
                    free(pool, s_res1, n(1))
                    pool.tensor_tensor(quad(x1_b[:, :]), quad(x1[:, :]), row(b1_row), ALU.add).then_inc(s_x1b, 1)
                if n.has(-1):
                    pool.wait_ge(s_xhi, n(-1))
                    pool.tensor_tensor(xT_lo[:, :], xT_in[1 - n.p][:, :], xT_hi[:, :].bitcast(F32), ALU.subtract).then_inc(s_xlo, 1)
                if n.has(3):
                    newton(3, n, 3)
            run(pool, step)


def kernel(**inputs):
    import numpy as _np
    import concourse.bacc as _bacc
    from concourse import mybir as _mybir
    from concourse.bass_utils import run_bass_kernel_spmd as _run

    def grouped(a):
        a = _np.asarray(a).reshape(GROUPS, Q, P, P)
        return _np.ascontiguousarray(a.transpose(0, 2, 1, 3)).reshape(GROUPS * P, W)

    def rows(a):
        return _np.ascontiguousarray(_np.asarray(a).T)

    x, adj = _np.asarray(inputs["x"]), _np.asarray(inputs["adj"])
    conv2 = _np.asarray(inputs["L2_gnn_conv2_w"])
    arrays = {
        "x": grouped(x),
        "xT": grouped(x.transpose(0, 2, 1)),
        "adj": grouped(adj),
        "adjT": grouped(adj.transpose(0, 2, 1)),
        "mask": _np.asarray(inputs["nodemask"]).reshape(GROUPS, W),
        "w0": _np.asarray(inputs["L0_gnn_W"]),
        "w1": _np.asarray(inputs["L1_gnn_weight"]),
        "b1": _np.asarray(inputs["L1_gnn_bias"]).reshape(1, P),
        "conv1": rows(_np.asarray(inputs["L2_gnn_conv1_w"]).reshape(P, P)),
        "conv2": _np.ascontiguousarray(conv2.transpose(1, 2, 0)).reshape(P, TAPS * P),
        "bn": _np.ascontiguousarray(_np.stack([_np.asarray(inputs[f"L2_gnn_bn{i}_{v}"])
                                               for i in (1, 2) for v in "gbmv"], axis=1)),
        "wih": rows(inputs["L2_gnn_w_ih"]),
        "whh": rows(inputs["L2_gnn_w_hh"]),
        "bih": rows(_np.asarray(inputs["L2_gnn_b_ih"]).reshape(3, P)),
        "bhh": rows(_np.asarray(inputs["L2_gnn_b_hh"]).reshape(3, P)),
        "wmsg": rows(inputs["L2_gnn_w_msg"]),
        "wse": rows(inputs["L2_gnn_w_se"]),
        "bmsg": _np.asarray(inputs["L2_gnn_b_msg"]).reshape(1, P),
        "bse": _np.asarray(inputs["L2_gnn_b_se"]).reshape(1, SE),
        "w3": rows(inputs["L3_gnn_W"]),
        "b3": _np.asarray(inputs["L3_gnn_b"]).reshape(1, P),
        "eye": _np.eye(P, dtype=_np.float32),
    }
    nc = _bacc.Bacc("TRN2", target_bir_lowering=False, num_devices=1)
    args = [nc.dram_tensor(f"in_{k}", a.shape, _mybir.dt.from_np(a.dtype), kind="ExternalInput").ap()
            for k, a in arrays.items()]
    args.append(nc.dram_tensor("out_0", (GROUPS * P, W), _mybir.dt.float32, kind="ExternalOutput").ap())
    four_gnn_layers(nc, *args)
    r = _run(nc, [{f"in_{k}": a for k, a in arrays.items()}], core_ids=[0])
    out = r.results[0]["out_0"].reshape(GROUPS, P, Q, P)
    return _np.ascontiguousarray(out.transpose(0, 2, 1, 3)).reshape(128, P, P)
```

```python
from contextlib import ExitStack

import concourse.bass as bass
from concourse import mybir

F32 = mybir.dt.float32
F32R = mybir.dt.float32r
I32 = mybir.dt.int32
ALU = mybir.AluOpType
ACT = mybir.ActivationFunctionType
AX = mybir.AxisListType

P = 128
Q = 4
W = Q * P
GROUPS = 128 // Q
TAPS = 17
PAD = TAPS // 2
PW = P + 2 * PAD
LAST_LAG = 3
FIRST_STEADY = 4
END_STEADY = GROUPS - 2
EPS = 1e-5
MASKED = 1e30
MAGIC = float(0x5F3759DF)
NEWTON = 3
LOADS = 4
NSTEP = {0: 3 * NEWTON, 1: 3 * NEWTON, 2: 3 * NEWTON, 3: 4 * NEWTON}
VEC_STEPS = 2 + 3 * NEWTON + 7

U_W0, U_CONV1, U_CONV2 = 0, 1, 2
U_IH_CONV, U_IH_NMP, U_HH = U_CONV2 + TAPS, U_CONV2 + TAPS + 3, U_CONV2 + TAPS + 6
UNITS = U_HH + 3
GATE_R, GATE_Z, GATE_N = 0, 1, 2
SE = 3
VW = 32


def four_gnn_layers(nc, x_d, xT_d, adj_d, adjT_d, mask_d, w0_d, w1_d, b1_d, conv1_d, conv2_d,
                    bn_d, wih_d, whh_d, bih_d, bhh_d, wmsg_d, wse_d, bmsg_d, bse_d, w3_d, b3_d,
                    eye_d, out_d):
    ctx = ExitStack()
    with ctx:
        def sb(name, cols, dt=F32):
            return ctx.enter_context(nc.sbuf_tensor(name, [P, *cols], dt))

        def sem(name):
            return ctx.enter_context(nc.semaphore(name))

        staging = sb("staging", [UNITS * P])
        w_hi = sb("w_hi", [UNITS * P], F32R)
        w_lo = sb("w_lo", [UNITS * P], F32R)
        w1 = sb("w1", [P])
        w3 = sb("w3", [P])
        w_msg = sb("w_msg", [P + SE])
        eye = sb("eye", [P])
        b1_row = sb("b1_row", [P])
        b3_row = sb("b3_row", [P])
        bmsg_row = sb("bmsg_row", [P])
        bse_row = sb("bse_row", [SE])
        bn = sb("bn", [8])
        bih = sb("bih", [3])
        bhh = sb("bhh", [3])
        aff = sb("aff", [4])
        gate_b = sb("gate_b", [4])
        tmp = sb("tmp", [8])
        dm_all = sb("dm_all", [GROUPS * Q])
        dm = sb("dm", [Q])

        x_in = [sb(f"x_in{p}", [W]) for p in range(2)]
        xT_in = [sb(f"xT_in{p}", [W]) for p in range(2)]
        adj_in = [sb(f"adj_in{p}", [W]) for p in range(2)]
        adjT_in = [sb(f"adjT_in{p}", [W]) for p in range(2)]
        mask_in = [sb(f"mask_in{p}", [W], I32) for p in range(2)]
        xT_hi = sb("xT_hi", [W], F32R)
        xT_lo = sb("xT_lo", [W], F32R)
        mask_add = sb("mask_add", [W])
        deg = sb("deg", [Q])
        inter = sb("inter", [W])
        logit = sb("logit", [W])
        logit_min = sb("logit_min", [Q])
        prob = sb("prob", [W])
        prob_sum = sb("prob_sum", [Q])
        prob_inv = sb("prob_inv", [Q])
        probT = sb("probT", [W])
        res0 = sb("res0", [W])
        x1 = sb("x1", [W])
        aggT = sb("aggT", [W])
        x1_b = sb("x1_b", [W])
        res1 = sb("res1", [W])
        x2 = sb("x2", [W])
        x2T = [sb(f"x2T{p}", [W]) for p in range(2)]
        x2T_hi = [sb(f"x2T_hi{p}", [W], F32R) for p in range(2)]
        x2T_lo = [sb(f"x2T_lo{p}", [W], F32R) for p in range(2)]
        x2T_b = sb("x2T_b", [W])
        h1 = sb("h1", [W])
        h1_hi = sb("h1_hi", [Q, PW], F32R)
        h1_lo = sb("h1_lo", [Q, PW], F32R)
        msg_b = sb("msg_b", [W])
        msg = sb("msg", [W])
        vl = sb("vl", [Q, VW])
        vr = sb("vr", [Q * (P + VW)])
        s_sq = sb("s_sq", [Q, SE])
        s_sum_t = sb("s_sum_t", [Q])
        vlT = sb("vlT", [P])
        vrT = sb("vrT", [W])
        near = sb("near", [W])
        near_adjT = sb("near_adjT", [W])
        nmp_hi = sb("nmp_hi", [W], F32R)
        nmp_lo = sb("nmp_lo", [W], F32R)
        conv = sb("conv", [W])
        conv_hi = sb("conv_hi", [W], F32R)
        conv_lo = sb("conv_lo", [W], F32R)
        gr = sb("gr", [W])
        gz = sb("gz", [W])
        gh = sb("gh", [W])
        gw = sb("gw", [W])
        gn = sb("gn", [W])
        gd = sb("gd", [W])
        y = sb("y", [W])
        x3 = sb("x3", [W])
        x3T = sb("x3T", [W])
        lin3 = sb("lin3", [W])
        lin3_d = sb("lin3_d", [W])
        res3 = sb("res3", [W])
        x4 = sb("x4", [W])
        adjT3 = [sb(f"adjT3{p}", [W]) for p in range(2)]
        stats = [sb(f"stats{i}", [Q, 6]) for i in range(4)]
        mv = [sb(f"mv{i}", [Q, 2]) for i in range(4)]
        var = [sb(f"var{i}", [2 * Q if i == 0 else Q]) for i in range(4)]
        rstd = [sb(f"rstd{i}", [2 * Q if i == 0 else Q]) for i in range(4)]
        nwt = [sb(f"nwt{i}", [2 * Q if i == 0 else Q]) for i in range(4)]
        neg_mean = [sb(f"neg_mean{i}", [Q]) for i in range(4)]
        shift = [sb(f"shift{i}", [Q]) for i in range(4)]

        def bank(name):
            return ctx.enter_context(nc.psum_tensor(name, [P, 512], F32))

        ps_a, ps_b, ps_c, ps_d = bank("ps_a"), bank("ps_b"), bank("ps_c"), bank("ps_d")
        ps_r, ps_z, ps_n, ps_h = bank("ps_r"), bank("ps_z"), bank("ps_n"), bank("ps_h")

        s_w = sem("s_w")
        s_whi, s_wlo = sem("s_whi"), sem("s_wlo")
        s_zero, s_const, s_vec = sem("s_zero"), sem("s_const"), sem("s_vec")
        s_loadT = [sem(f"s_loadT{p}") for p in range(2)]
        s_load = [sem(f"s_load{p}") for p in range(2)]
        s_adj3 = [sem(f"s_adj3{p}") for p in range(2)]
        s_store = sem("s_store")
        (s_xhi, s_xlo, s_mask, s_deg, s_interps, s_inter, s_scoreps, s_prod, s_logit, s_prob,
         s_probTps, s_probT, s_inv, s_out0ps, s_res0, s_x1, s_dm) = (sem(x) for x in (
            "s_xhi", "s_xlo", "s_mask", "s_deg", "s_interps", "s_inter", "s_scoreps", "s_prod",
            "s_logit", "s_prob", "s_probTps", "s_probT", "s_inv", "s_out0ps", "s_res0", "s_x1",
            "s_dm"))
        (s_aggps, s_agg, s_x1b, s_out1ps, s_res1, s_x2) = (sem(x) for x in (
            "s_aggps", "s_agg", "s_x1b", "s_out1ps", "s_res1", "s_x2"))
        (s_x2Tps, s_x2T, s_x2Thi, s_x2Tlo, s_x2Tb, s_conv1ps, s_h1, s_h1hi, s_h1lo, s_msgps, s_msgb,
         s_msg, s_emb, s_sq_sem, s_sum, s_v, s_vps, s_vlT, s_vrT, s_distps, s_near, s_nadj, s_nmpps,
         s_nmphi, s_nmplo, s_conv2ps, s_conv, s_convhi, s_convlo) = (sem(x) for x in (
            "s_x2Tps", "s_x2T", "s_x2Thi", "s_x2Tlo", "s_x2Tb", "s_conv1ps", "s_h1", "s_h1hi",
            "s_h1lo", "s_msgps", "s_msgb", "s_msg", "s_emb", "s_sq", "s_sum", "s_v", "s_vps",
            "s_vlT", "s_vrT", "s_distps", "s_near", "s_nadj", "s_nmpps", "s_nmphi", "s_nmplo",
            "s_conv2ps", "s_conv", "s_convhi", "s_convlo"))
        (s_ghps, s_gateps, s_gr, s_gh, s_gz, s_gw, s_gw2, s_gn, s_gd, s_ge, s_y) = (
            sem(x) for x in ("s_ghps", "s_gateps", "s_gr", "s_gh", "s_gz", "s_gw", "s_gw2",
                             "s_gn", "s_gd", "s_ge", "s_y"))
        (s_yTps, s_x3, s_x3Tps, s_x3T, s_lin3ps, s_lin3, s_dmc, s_lin3d, s_out3ps, s_relu3,
         s_res3, s_x4) = (sem(x) for x in (
            "s_yTps", "s_x3", "s_x3Tps", "s_x3T", "s_lin3ps", "s_lin3", "s_dmc", "s_lin3d",
            "s_out3ps", "s_relu3", "s_res3", "s_x4"))
        s_stats = [sem(f"s_stats{i}") for i in range(4)]
        s_mv = [sem(f"s_mv{i}") for i in range(4)]
        s_var = [sem(f"s_var{i}") for i in range(4)]
        s_guess = [sem(f"s_guess{i}") for i in range(4)]
        s_rstd = [sem(f"s_rstd{i}") for i in range(4)]
        s_shift = [sem(f"s_shift{i}") for i in range(4)]

        s_sq_, s_norm = s_sq_sem, sem("s_norm")

        def vr_of(a, b):
            return vr[:, :].rearrange("p (q c) -> p q c", q=Q)[:, :, a:b]

        def col(tile, q):
            return tile[:, q * P:(q + 1) * P]

        def quad(ap):
            return ap.rearrange("p (q n) -> p q n", q=Q)

        def row(tile, n=P):
            return tile[:, 0:n].unsqueeze(1).broadcast_to((P, Q, n))

        def per_graph(tile):
            return tile[:, 0:Q].unsqueeze(2).broadcast_to((P, Q, P))

        class Step:

            def __init__(self, eng, even, u, kept):
                self.eng, self.even, self.u, self.kept = eng, even, u, kept
                self.fixed = isinstance(even, int)

            def p(self, lag):
                return (self.u + lag) % 2

            def has(self, lag):
                return not self.fixed or 0 <= self.even + self.u - lag < GROUPS

            def __call__(self, lag, k=1, less=0):
                c = self.u - lag + 1
                if self.fixed:
                    return k * min(self.even + c, GROUPS) - less
                if k not in self.kept:
                    self.kept[k] = {}
                if k == 1:
                    if c not in self.kept[k]:
                        self.kept[k][c] = self.eng.snap(self.even + c)
                    return self.kept[k][c]
                if 0 not in self.kept[k]:
                    self.kept[k][0] = self.eng.snap(self.even * k)
                return self.kept[k][0] + (k * c - less)

            def halves(self, lag, k):
                c = (self.u - lag) // 2 + 1
                if self.fixed:
                    return k * (self.even // 2 + c)
                if ("h", k) not in self.kept:
                    self.kept["h", k] = self.eng.snap(self.even * (k // 2))
                return self.kept["h", k] + k * c

            def at(self, lag, unit):
                return (self.even + (self.u - lag)) * unit

        def free(eng, sema, value):
            if not isinstance(value, int) or value > 0:
                eng.wait_ge(sema, value)

        def run(eng, step):
            for t in range(-1, FIRST_STEADY):
                step(Step(eng, t - t % 2, t % 2, {}))
            with eng.Fori(FIRST_STEADY // 2, END_STEADY // 2) as pair:
                kept, even = {}, pair * 2
                for u in range(2):
                    step(Step(eng, even, u, kept))
            for t in range(END_STEADY, GROUPS + LAST_LAG):
                step(Step(eng, t - t % 2, t % 2, {}))

        block = ctx.enter_context(nc.Block())

        @block.sync
        def _(sp):
            def load(g, p):
                rows = bass.ds(g * P, P)
                sp.dma_start(xT_in[p][:, :], xT_d[rows, :]).then_inc(s_load[p], 16)
                sp.dma_start(adj_in[p][:, :], adj_d[rows, :]).then_inc(s_load[p], 16)
                sp.dma_start(mask_in[p][:, :], mask_d[bass.ds(g, 1), :].broadcast_to((P, W))).then_inc(s_load[p], 16)
                sp.dma_start(x_in[p][:, :], x_d[rows, :]).then_inc(s_load[p], 16)

            def load_adjT(g, p):
                sp.dma_start(adjT_in[p][:, :], adjT_d[bass.ds(g * P, P), :]).then_inc(s_loadT[p], 16)

            load(0, 0)
            units = [(w0_d, U_W0, 1), (conv1_d, U_CONV1, 1), (conv2_d, U_CONV2, TAPS),
                     (wih_d[0:P, :], U_IH_CONV, 3), (wih_d[P:2 * P, :], U_IH_NMP, 3), (whh_d, U_HH, 3)]
            for src, u0, k in units:
                sp.dma_start(staging[:, u0 * P:(u0 + k) * P], src).then_inc(s_w, 16)
            for dst, src in [(w1[:, :], w1_d), (w3[:, :], w3_d), (w_msg[:, 0:P], wmsg_d),
                             (w_msg[:, P:P + SE], wse_d), (eye[:, :], eye_d),
                             (b1_row[:, :], b1_d.broadcast_to((P, P))),
                             (b3_row[:, :], b3_d.broadcast_to((P, P))),
                             (bmsg_row[:, :], bmsg_d.broadcast_to((P, P))),
                             (bse_row[:, :], bse_d.broadcast_to((P, SE))),
                             (bn[:, :], bn_d), (bih[:, :], bih_d), (bhh[:, :], bhh_d)]:
                sp.dma_start(dst, src).then_inc(s_const, 16)
            load(1, 1)
            load_adjT(0, 0)

            def held():
                sp.nop(nofuse=True)

            def step(n):
                if n.has(1):
                    free(sp, s_out3ps, n(3))
                    held()
                    sp.wait_ge(s_aggps, n(1))
                    sp.dma_start(adjT3[n.p(1)][:, :], adjT_in[n.p(1)][:, :]).then_inc(s_adj3[n.p(1)], 16)
                if n.has(0) and n.has(-2):
                    sp.wait_ge(s_res0, n(0))
                    held()
                    load(n.even + (n.u + 2), n.p(0))
                if n.has(-1) and n.has(0):
                    if n.has(1):
                        sp.wait_ge(s_nadj, n(1))
                        held()
                        sp.wait_ge(s_adj3[n.p(1)], n.halves(1, 16))
                        held()
                    load_adjT(n.even + (n.u + 1), n.p(-1))
                if n.has(3):
                    sp.wait_ge(s_x4, n(3))
                    held()
                    sp.dma_start(out_d[bass.ds(n.at(3, P), P), :], x4[:, :]).then_inc(s_store, 16)
            run(sp, step)
            sp.wait_ge(s_store, 16 * GROUPS)

        @block.tensor
        def _(pe):
            def split_product(ps, unit, hi, lo, start, stop):
                wh, wl = w_hi[:, unit * P:(unit + 1) * P], w_lo[:, unit * P:(unit + 1) * P]
                pe.matmul(ps, wh, hi, start=start, stop=False)
                pe.matmul(ps, wh, lo, start=False, stop=False)
                return pe.matmul(ps, wl, hi, start=False, stop=stop)

            def taps(n, a, b):
                if not n.has(1):
                    return
                if a == 0:
                    pe.wait_ge(s_h1hi, n(1))
                    pe.wait_ge(s_h1lo, n(1))
                    free(pe, s_conv, n(2))
                for k in range(a, b):
                    mm = split_product(ps_n[:, :], U_CONV2 + k, h1_hi[:, :, k:k + P],
                                       h1_lo[:, :, k:k + P], k == 0, k == TAPS - 1)
                if b == TAPS:
                    mm.then_inc(s_conv2ps, 1)

            pe.wait_ge(s_whi, 1)
            pe.wait_ge(s_wlo, 1)
            pe.wait_ge(s_const, 16 * 12)

            def step(n):
                if n.has(2):
                    xh, xl = x2T_hi[n.p(2)][:, :], x2T_lo[n.p(2)][:, :]
                    free(pe, s_gr, n(3))
                    free(pe, s_gz, n(3))
                    pe.wait_ge(s_vrT, n(2))
                    split_product(ps_r[:, :], U_HH + GATE_R, xh, xl, True, False)
                    split_product(ps_z[:, :], U_HH + GATE_Z, xh, xl, True, False)
                    split_product(ps_h[:, :], U_HH + GATE_N, xh, xl, True, True).then_inc(s_ghps, 1)
                if n.has(0):
                    pe.wait_ge(s_prob, n(0))
                    for q in range(Q):
                        mm = pe.transpose(col(ps_b, q), col(prob, q), eye[:, :])
                    mm.then_inc(s_probTps, 1)
                if n.has(1):
                    pe.wait_ge(s_x2, n(1))
                    free(pe, s_nmphi, n(2))
                    free(pe, s_nmplo, n(2))
                    for q in range(Q):
                        mm = pe.transpose(col(ps_d, q), col(x2, q), eye[:, :])
                    mm.then_inc(s_x2Tps, 1)
                if n.has(2):
                    pe.wait_ge(s_nmplo, n(2))
                    split_product(ps_r[:, :], U_IH_NMP + GATE_R, nmp_hi[:, :], nmp_lo[:, :], False, False)
                    split_product(ps_z[:, :], U_IH_NMP + GATE_Z, nmp_hi[:, :], nmp_lo[:, :], False, False)
                if n.has(0):
                    pe.wait_ge(s_probT, n(0))
                    free(pe, s_res1, n(1))
                    for q in range(Q):
                        mm = pe.matmul(col(ps_a, q), col(probT, q), col(x_in[n.p(0)], q), start=True, stop=True)
                    mm.then_inc(s_out0ps, 1)
                if n.has(3):
                    pe.wait_ge(s_lin3d, n(3))
                    pe.wait_ge(s_adj3[n.p(3)], n.halves(3, 16))
                    for q in range(Q):
                        mm = pe.matmul(col(ps_c, q), col(adjT3[n.p(3)], q), col(lin3_d, q), start=True, stop=True)
                    mm.then_inc(s_out3ps, 1)
                if n.has(2):
                    pe.wait_ge(s_convlo, n(2))
                    split_product(ps_r[:, :], U_IH_CONV + GATE_R, conv_hi[:, :], conv_lo[:, :], False, True).then_inc(s_gateps, 1)
                if n.has(1):
                    pe.wait_ge(s_x2Tb, n(1))
                    pe.wait_ge(s_x2Tlo, n(1))
                    split_product(ps_d[:, :], U_CONV1, x2T_hi[n.p(1)][:, :], x2T_lo[n.p(1)][:, :],
                                  True, True).then_inc(s_conv1ps, 1)
                if n.has(2):
                    pe.wait_ge(s_gh, n(2))
                    split_product(ps_h[:, :], U_IH_NMP + GATE_N, nmp_hi[:, :], nmp_lo[:, :], True, False)
                    split_product(ps_h[:, :], U_IH_CONV + GATE_N, conv_hi[:, :], conv_lo[:, :], False, True).then_inc(s_gateps, 1)
                if n.has(-1):
                    pe.wait_ge(s_xhi, n(-1))
                    pe.wait_ge(s_xlo, n(-1))
                    free(pe, s_probT, n(0))
                    split_product(ps_b[:, :], U_W0, xT_hi[:, :], xT_lo[:, :], True, True).then_inc(s_interps, 1)
                if n.has(1):
                    pe.wait_ge(s_res0, n(0))
                    pe.wait_ge(s_h1, n(1))
                    for q in range(Q):
                        dst = (ps_a if q < 2 else ps_d)[:, (q % 2) * (P + SE):(q % 2 + 1) * (P + SE)]
                        mm = pe.matmul(dst, col(x2T[n.p(1)], q), w_msg[:, :], start=True, stop=True)
                    mm.then_inc(s_msgps, 1)
                if n.has(2):
                    split_product(ps_z[:, :], U_IH_CONV + GATE_Z, conv_hi[:, :], conv_lo[:, :], False, True).then_inc(s_gateps, 1)
                if n.has(-1):
                    pe.wait_ge(s_inter, n(-1))
                    for q in range(Q):
                        mm = pe.matmul(col(ps_b, q), col(inter, q), col(xT_in[n.p(-1)], q), start=True, stop=True)
                    mm.then_inc(s_scoreps, 1)
                taps(n, 0, 4)
                if n.has(1):
                    pe.wait_ge(s_v, n(1))
                    pe.wait_ge(s_msgb, n(1))
                    free(pe, s_gw2, n(2))
                    pe.transpose(ps_d[:, 0:P], vl[:, :, :].rearrange("p q c -> p (q c)"), eye[:, :])
                    for q in range(Q):
                        mm = pe.transpose(col(ps_h, q), vr[:, q * P:(q + 1) * P], eye[:, :])
                    mm.then_inc(s_vps, 1)
                taps(n, 4, 6)
                if n.has(2):
                    pe.wait_ge(s_y, n(2))
                    free(pe, s_relu3, n(3))
                    for q in range(Q):
                        mm = pe.transpose(col(ps_c, q), col(y, q), eye[:, :])
                    mm.then_inc(s_yTps, 1)
                if n.has(1):
                    pe.wait_ge(s_vrT, n(1))
                    pe.matmul(ps_d[:, :], vlT[:, :], vrT[:, :], start=True, stop=True).then_inc(s_distps, 1)
                taps(n, 6, 9)
                if n.has(0):
                    pe.wait_ge(s_x1, n(0))
                    free(pe, s_msgb, n(1))
                    pe.wait_ge(s_loadT[n.p(0)], n.halves(0, 16))
                    for q in range(Q):
                        mm = pe.matmul(col(ps_a, q), col(x1, q),
                                       col(adjT_in[n.p(0)], q), start=True, stop=True)
                    mm.then_inc(s_aggps, 1)
                taps(n, 9, 11)
                if n.has(0):
                    pe.wait_ge(s_agg, n(0))
                    for q in range(Q):
                        mm = pe.matmul(col(ps_a, q), col(aggT, q), w1[:, :], start=True, stop=True)
                    mm.then_inc(s_out1ps, 1)
                taps(n, 11, 12)
                if n.has(1):
                    pe.wait_ge(s_nadj, n(1))
                    pe.wait_ge(s_msg, n(1))
                    for q in range(Q):
                        mm = pe.matmul(col(ps_d, q), col(msg, q), col(near_adjT, q), start=True, stop=True)
                    mm.then_inc(s_nmpps, 1)
                taps(n, 12, 15)
                if n.has(2):
                    pe.wait_ge(s_x3, n(2))
                    for q in range(Q):
                        mm = pe.transpose(col(ps_c, q), col(x3, q), eye[:, :])
                    mm.then_inc(s_x3Tps, 1)
                taps(n, 15, TAPS)
                if n.has(2):
                    pe.wait_ge(s_x3T, n(2))
                    for q in range(Q):
                        mm = pe.matmul(col(ps_c, q), col(x3T, q), w3[:, :], start=True, stop=True)
                    mm.then_inc(s_lin3ps, 1)
            run(pe, step)

        @block.scalar
        def _(act):
            act.wait_ge(s_w, 16 * 6)
            act.copy(w_hi[:, :], staging[:, :]).then_inc(s_whi, 1)

            def apply(i, out, src, n, lag, done):
                act.wait_ge(s_shift[i], n(lag))
                for q in range(Q):
                    ins = act.activation(col(out, q), col(src, q), ACT.Identity, bias=shift[i][:, q:q + 1],
                                         scale=rstd[i][:, q:q + 1])
                ins.then_inc(done, 1)

            act.wait_ge(s_vec, VEC_STEPS)

            def step(n):
                if n.has(0):
                    act.wait_ge(s_probTps, n(0))
                    free(act, s_out0ps, n(1))
                    act.copy(probT[:, :], ps_b[:, :]).then_inc(s_probT, 1)
                if n.has(1):
                    act.wait_ge(s_x2Tps, n(1))
                    free(act, s_y, n(3))
                    act.copy(x2T[n.p(1)][:, :], ps_d[:, :]).then_inc(s_x2T, 1)
                if n.has(2):
                    act.wait_ge(s_conv, n(2))
                    free(act, s_gateps, n(3, 3))
                    act.activation(conv_hi[:, :], conv[:, :], ACT.Relu).then_inc(s_convhi, 1)
                if n.has(1):
                    free(act, s_ghps, n(3))
                    act.copy(x2T_hi[n.p(1)][:, :], ps_d[:, :]).then_inc(s_x2Thi, 1)
                if n.has(2):
                    act.wait_ge(s_ghps, n(2))
                    free(act, s_gw, n(3))
                    act.activation(gh[:, :], ps_h[:, :], ACT.Identity, bias=gate_b[:, 2:3], scale=0.5).then_inc(s_gh, 1)
                if n.has(1):
                    free(act, s_conv, n(2))
                    act.activation(x2T_b[:, :], ps_d[:, :], ACT.Identity, bias=aff[:, 3:4]).then_inc(s_x2Tb, 1)
                if n.has(-1):
                    act.wait_ge(s_load[n.p(-1)], n.halves(-1, 16 * LOADS))
                    free(act, s_interps, n(0))
                    act.copy(xT_hi[:, :], xT_in[n.p(-1)][:, :]).then_inc(s_xhi, 1)
                if n.has(2):
                    act.wait_ge(s_gateps, n(2, 3, 2))
                    free(act, s_gw, n(3))
                    act.activation(gr[:, :], ps_r[:, :], ACT.Tanh, bias=gate_b[:, 0:1], scale=0.5).then_inc(s_gr, 1)
                if n.has(1):
                    act.wait_ge(s_conv1ps, n(1))
                    free(act, s_h1lo, n(2))
                    act.activation(h1[:, :], ps_d[:, :], ACT.Relu, bias=aff[:, 2:3], scale=aff[:, 0:1]).then_inc(s_h1, 1)
                    act.wait_ge(s_h1, n(1))
                    free(act, s_conv2ps, n(2))
                    act.copy(h1_hi[:, :, PAD:PAD + P], quad(h1[:, :])).then_inc(s_h1hi, 1)
                if n.has(-1):
                    act.wait_ge(s_interps, n(-1))
                    free(act, s_scoreps, n(0))
                    act.mul(inter[:, :], ps_b[:, :], -1.0).then_inc(s_inter, 1)
                if n.has(2):
                    act.wait_ge(s_gw2, n(2))
                    free(act, s_gd, n(3))
                    act.activation(gn[:, :], gw[:, :], ACT.Tanh, bias=gate_b[:, 3:4]).then_inc(s_gn, 1)
                    act.wait_ge(s_gateps, n(2, 3))
                    free(act, s_ge, n(3))
                    act.activation(gz[:, :], ps_z[:, :], ACT.Tanh, bias=gate_b[:, 1:2], scale=0.5).then_inc(s_gz, 1)
                if n.has(1):
                    act.wait_ge(s_vps, n(1))
                    free(act, s_distps, n(2))
                    act.copy(vlT[:, :], ps_d[:, 0:P]).then_inc(s_vlT, 1)
                    act.copy(vrT[:, :], ps_h[:, :]).then_inc(s_vrT, 1)
                    act.wait_ge(s_msgb, n(1))
                    free(act, s_nmpps, n(2))
                    act.activation(msg[:, :], msg_b[:, :], ACT.Relu).then_inc(s_msg, 1)
                if n.has(0):
                    free(act, s_aggps, n(1))
                    free(act, s_x1b, n(1))
                    apply(0, x1, res0, n, 0, s_x1)
                if n.has(1):
                    act.wait_ge(s_distps, n(1))
                    free(act, s_nadj, n(2))
                    act.activation(near[:, :], ps_d[:, :], ACT.Exp).then_inc(s_near, 1)
                if n.has(0):
                    act.wait_ge(s_aggps, n(0))
                    free(act, s_out1ps, n(1))
                    act.copy(aggT[:, :], ps_a[:, :]).then_inc(s_agg, 1)
                if n.has(-1):
                    act.wait_ge(s_logit, n(-1))
                    free(act, s_probTps, n(0))
                    free(act, s_inv, n(0))
                    for q in range(Q):
                        ins = act.activation(col(prob, q), col(logit, q), ACT.Exp, bias=logit_min[:, q:q + 1],
                                             scale=-1.0, accum_out=prob_sum[:, q:q + 1])
                    ins.then_inc(s_prob, 1)
                if n.has(2):
                    free(act, s_res3, n(3))
                    apply(2, x3, ps_c, n, 2, s_x3)
                    act.wait_ge(s_x3Tps, n(2))
                    free(act, s_lin3ps, n(3))
                    act.copy(x3T[:, :], ps_c[:, :]).then_inc(s_x3T, 1)
                if n.has(1):
                    act.wait_ge(s_nmpps, n(1))
                    free(act, s_gateps, n(2, 3))
                    act.copy(nmp_hi[:, :], ps_d[:, :]).then_inc(s_nmphi, 1)
                if n.has(0):
                    free(act, s_x2Tps, n(1))
                    apply(1, x2, res1, n, 0, s_x2)
            run(act, step)

        @block.vector
        def _(dve):
            def held():
                dve.nop(nofuse=True)

            for tile in (h1_hi, h1_lo):
                dve.memset(tile[:, :, :].bitcast(F32), 0.0).then_inc(s_zero, 1)
            dve.memset(vl[:, :, :], 0.0).then_inc(s_zero, 1)
            dve.memset(vr[:, :], 0.0).then_inc(s_zero, 1)
            dve.wait_ge(s_zero, 4)
            dve.memset(vl[:, :, 4:5], 1.0).then_inc(s_zero, 1)
            dve.memset(vr_of(3, 4), -1.0).then_inc(s_zero, 1)

            vec = [0]

            def chain(ins):
                ins.then_inc(s_vec, 1)
                vec[0] += 1
                dve.wait_ge(s_vec, vec[0])

            two = lambda tile, a: tile[:, a:a + 5:4]
            dve.wait_ge(s_const, 16 * 12)
            v, g, a = tmp[:, 0:2], tmp[:, 2:4], tmp[:, 4:6]
            chain(dve.tensor_scalar(v, two(bn, 3), EPS, None, ALU.add))
            chain(dve.tensor_scalar(g.bitcast(I32), v.bitcast(I32), -0.5, MAGIC, ALU.mult, ALU.add))
            for _ in range(NEWTON):
                chain(dve.scalar_tensor_tensor(out=a, in0=g, scalar=-0.5, in1=g, op0=ALU.mult, op1=ALU.mult))
                chain(dve.tensor_tensor(a, a, v, ALU.mult))
                chain(dve.scalar_tensor_tensor(out=g, in0=a, scalar=1.5, in1=g, op0=ALU.add, op1=ALU.mult))
            chain(dve.tensor_tensor(aff[:, 0:2], two(bn, 0), g, ALU.mult))
            chain(dve.tensor_tensor(a, two(bn, 2), aff[:, 0:2], ALU.mult))
            chain(dve.tensor_tensor(aff[:, 2:4], two(bn, 1), a, ALU.subtract))
            chain(dve.tensor_tensor(a, bih[:, 0:2], bhh[:, 0:2], ALU.add))
            chain(dve.tensor_scalar(gate_b[:, 0:2], a, 0.5, None, ALU.mult))
            chain(dve.tensor_scalar(gate_b[:, 2:3], bhh[:, 2:3], 0.5, None, ALU.mult))
            chain(dve.tensor_copy(gate_b[:, 3:4], bih[:, 2:3]))
            assert vec[0] == VEC_STEPS

            dve.wait_ge(s_whi, 1)
            dve.tensor_tensor(w_lo[:, :], staging[:, :], w_hi[:, :].bitcast(F32), ALU.subtract).then_inc(s_wlo, 1)

            def look(i, src, n, lag):
                for q in range(Q):
                    ins = dve.bn_stats(stats[i][:, q, :], col(src, q))
                ins.then_inc(s_stats[i], 1)

            def moments(i, n, lag):
                dve.wait_ge(s_stats[i], n(lag))
                held()
                for q in range(Q):
                    ins = dve.bn_aggr(mv[i][:, q, :], stats[i][:, q, :])
                ins.then_inc(s_mv[i], 1)

            def spread(i, n, lag):
                dve.wait_ge(s_mv[i], n(lag))
                eps = 4 * EPS if i == 2 else EPS
                dve.tensor_scalar(neg_mean[i][:, :], mv[i][:, :, 0], -1.0, None, ALU.mult)
                dve.tensor_scalar(var[i][:, 0:Q], mv[i][:, :, 1], eps, None, ALU.add).then_inc(s_var[i], 1)

            def guess(i, n, lag):
                dve.wait_ge(s_var[i], n(lag))
                dve.tensor_scalar(rstd[i][:, :].bitcast(I32), var[i][:, :].bitcast(I32), -0.5, MAGIC,
                                  ALU.mult, ALU.add).then_inc(s_guess[i], 1)

            def apply(i, out, src, n, lag, done):
                dve.wait_ge(s_rstd[i], n(lag, NSTEP[i]))
                for q in range(Q):
                    ins = dve.tensor_scalar(col(out, q), col(src, q), mv[i][:, q, 0:1], rstd[i][:, q:q + 1],
                                            ALU.subtract, ALU.mult)
                ins.then_inc(done, 1)

            def newton(i, n, lag, first=0, last=NEWTON):
                v, y_, a = var[i][:, :], rstd[i][:, :], nwt[i][:, :]
                for k in range(first, last):
                    left = NSTEP[i] - 3 * k
                    if k == 0:
                        dve.wait_ge(s_guess[i], n(lag))
                    else:
                        dve.wait_ge(s_rstd[i], n(lag, NSTEP[i], left))
                    dve.scalar_tensor_tensor(out=a, in0=y_, scalar=-0.5, in1=y_, op0=ALU.mult,
                                             op1=ALU.mult).then_inc(s_rstd[i], 1)
                    dve.wait_ge(s_rstd[i], n(lag, NSTEP[i], left - 1))
                    dve.tensor_tensor(a, a, v, ALU.mult).then_inc(s_rstd[i], 1)
                    dve.wait_ge(s_rstd[i], n(lag, NSTEP[i], left - 2))
                    dve.scalar_tensor_tensor(out=y_, in0=a, scalar=1.5, in1=y_, op0=ALU.add,
                                             op1=ALU.mult).then_inc(s_rstd[i], 1)

            def message_part(h):
                return (ps_a, ps_d)[h][:, 0:2 * (P + SE)].rearrange("p (q c) -> p q c", q=2)

            def step(n):
                if n.has(2):
                    dve.wait_ge(s_conv2ps, n(2))
                    dve.wait_ge(s_x2Tb, n(2))
                    free(dve, s_convhi, n(3))
                    free(dve, s_convlo, n(3))
                    dve.scalar_tensor_tensor(out=conv[:, :], in0=ps_n[:, :], scalar=aff[:, 1:2], in1=x2T_b[:, :],
                                             op0=ALU.mult, op1=ALU.add).then_inc(s_conv, 1)
                if n.has(-1):
                    dve.wait_ge(s_load[n.p(-1)], n.halves(-1, 16 * LOADS))
                    free(dve, s_logit, n(0))
                    dve.tensor_scalar(mask_add[:, :], mask_in[n.p(-1)][:, :], 0, MASKED, ALU.is_equal, ALU.mult).then_inc(s_mask, 1)
                if n.has(2):
                    dve.wait_ge(s_convhi, n(2))
                    free(dve, s_gateps, n(3, 3))
                    dve.scalar_tensor_tensor(out=conv_lo[:, :], in0=conv[:, :], scalar=0.0, in1=conv_hi[:, :].bitcast(F32),
                                             op0=ALU.max, op1=ALU.subtract).then_inc(s_convlo, 1)
                if n.has(1):
                    dve.wait_ge(s_x2Thi, n(1))
                    free(dve, s_ghps, n(3))
                    dve.tensor_tensor(x2T_lo[n.p(1)][:, :], x2T[n.p(1)][:, :], x2T_hi[n.p(1)][:, :].bitcast(F32),
                                      ALU.subtract).then_inc(s_x2Tlo, 1)
                if n.has(0):
                    dve.wait_ge(s_prob, n(0))
                    dve.reciprocal(prob_inv[:, :], prob_sum[:, :]).then_inc(s_inv, 1)
                if n.has(3):
                    dve.wait_ge(s_out3ps, n(3))
                    dve.wait_ge(s_dmc, n(3))
                    free(dve, s_x4, n(4))
                    dve.scalar_tensor_tensor(out=quad(res3[:, :]), in0=quad(ps_c[:, :]), scalar=0.0, in1=per_graph(dm),
                                             op0=ALU.max, op1=ALU.mult).then_inc(s_relu3, 1)
                if n.has(0):
                    dve.wait_ge(s_out0ps, n(0))
                    dve.wait_ge(s_inv, n(0))
                    free(dve, s_x1, n(1))
                    for q in range(Q):
                        ins = dve.scalar_tensor_tensor(out=col(res0, q), in0=col(ps_a, q), scalar=prob_inv[:, q:q + 1],
                                                       in1=col(x_in[n.p(0)], q), op0=ALU.mult, op1=ALU.add)
                    ins.then_inc(s_res0, 1)
                if n.has(2):
                    dve.wait_ge(s_gr, n(2))
                    dve.wait_ge(s_gh, n(2))
                    free(dve, s_gn, n(3))
                    dve.scalar_tensor_tensor(out=gw[:, :], in0=gr[:, :], scalar=1.0, in1=gh[:, :],
                                             op0=ALU.add, op1=ALU.mult).then_inc(s_gw, 1)
                if n.has(0):
                    dve.wait_ge(s_deg, n(0))
                    dve.scalar_tensor_tensor(out=var[0][:, Q:2 * Q], in0=deg[:, :], scalar=0.0, in1=deg[:, :],
                                             op0=ALU.is_equal, op1=ALU.add)
                    dve.wait_ge(s_res0, n(0))
                    look(0, res0, n, 0)
                if n.has(2):
                    dve.wait_ge(s_gateps, n(2, 3, 1))
                    dve.wait_ge(s_gw, n(2))
                    dve.tensor_tensor(gw[:, :], gw[:, :], ps_h[:, :], ALU.add).then_inc(s_gw2, 1)
                if n.has(1):
                    dve.wait_ge(s_msgps, n(1))
                    free(dve, s_vps, n(2))
                    for h in range(2):
                        ins = dve.tensor_tensor(vl[:, 2 * h:2 * h + 2, 0:SE], message_part(h)[:, :, P:P + SE],
                                                bse_row[:, :].unsqueeze(1).broadcast_to((P, 2, SE)), ALU.add)
                    ins.then_inc(s_emb, 1)
                if n.has(3):
                    dve.wait_ge(s_res3, n(3))
                    look(3, res3, n, 3)
                if n.has(2):
                    free(dve, s_lin3d, n(3))
                    free(dve, s_relu3, n(3))
                    dve.tensor_copy(dm[:, :], dm_all[:, bass.ds(n.at(2, Q), Q)]).then_inc(s_dmc, 1)
                if n.has(0):
                    moments(0, n, 0)
                if n.has(1):
                    free(dve, s_msg, n(2))
                    for h in range(2):
                        ins = dve.tensor_tensor(quad(msg_b[:, :])[:, 2 * h:2 * h + 2, :], message_part(h)[:, :, 0:P],
                                                bmsg_row[:, :].unsqueeze(1).broadcast_to((P, 2, P)), ALU.add)
                    ins.then_inc(s_msgb, 1)
                if n.has(3):
                    moments(3, n, 3)
                if n.has(0):
                    spread(0, n, 0)
                if n.has(2):
                    dve.wait_ge(s_gd, n(2))
                    dve.wait_ge(s_gz, n(2))
                    dve.scalar_tensor_tensor(out=gd[:, :], in0=gz[:, :], scalar=-1.0, in1=gd[:, :],
                                             op0=ALU.add, op1=ALU.mult).then_inc(s_ge, 1)
                if n.has(0):
                    guess(0, n, 0)
                if n.has(-1):
                    dve.wait_ge(s_scoreps, n(-1))
                    free(dve, s_prob, n(0))
                    dve.tensor_tensor(logit[:, :], ps_b[:, :], adj_in[n.p(-1)][:, :], ALU.mult).then_inc(s_prod, 1)
                if n.has(2):
                    dve.wait_ge(s_ge, n(2))
                    free(dve, s_yTps, n(3))
                    dve.scalar_tensor_tensor(out=y[:, :], in0=x2T[n.p(2)][:, :], scalar=4.0, in1=gd[:, :],
                                             op0=ALU.mult, op1=ALU.add).then_inc(s_y, 1)
                if n.has(0):
                    newton(0, n, 0, 0, 3)
                if n.has(-1):
                    dve.wait_ge(s_prod, n(-1))
                    dve.wait_ge(s_mask, n(-1))
                    held()
                    for q in range(Q):
                        ins = dve.tensor_tensor_reduce(col(logit, q), col(logit, q), col(mask_add, q), 1.0, MASKED * 2,
                                                       ALU.add, ALU.min, logit_min[:, q:q + 1])
                    ins.then_inc(s_logit, 1)
                if n.has(2):
                    dve.wait_ge(s_yTps, n(2))
                    held()
                    look(2, ps_c, n, 2)
                    moments(2, n, 2)
                    spread(2, n, 2)
                    guess(2, n, 2)
                if n.has(3):
                    spread(3, n, 3)
                if n.has(2):
                    newton(2, n, 2, 0, 2)
                if n.has(3):
                    guess(3, n, 3)
                if n.has(0):
                    dve.wait_ge(s_rstd[0], n(0, NSTEP[0]))
                    dve.scalar_tensor_tensor(out=dm_all[:, bass.ds(n.at(0, Q), Q)], in0=deg[:, :], scalar=0.0,
                                             in1=rstd[0][:, Q:2 * Q], op0=ALU.not_equal, op1=ALU.mult).then_inc(s_dm, 1)
                if n.has(1):
                    dve.wait_ge(s_near, n(1))
                    free(dve, s_nmpps, n(2))
                    dve.tensor_tensor(near_adjT[:, :], near[:, :], adjT_in[n.p(1)][:, :], ALU.mult).then_inc(s_nadj, 1)
                if n.has(2):
                    newton(2, n, 2, 2, 3)
                if n.has(0):
                    dve.wait_ge(s_out1ps, n(0))
                    dve.wait_ge(s_x1b, n(0))
                    free(dve, s_x2, n(1))
                    dve.tensor_tensor(res1[:, :], ps_a[:, :], x1_b[:, :], ALU.add).then_inc(s_res1, 1)
                    dve.wait_ge(s_res1, n(0))
                    look(1, res1, n, 0)
                    moments(1, n, 0)
                    spread(1, n, 0)
                    guess(1, n, 0)
                    newton(1, n, 0, 0, 3)
                if n.has(1):
                    dve.wait_ge(s_nmphi, n(1))
                    free(dve, s_gateps, n(2, 3))
                    dve.tensor_tensor(nmp_lo[:, :], ps_d[:, :], nmp_hi[:, :].bitcast(F32), ALU.subtract).then_inc(s_nmplo, 1)
                if n.has(-1):
                    free(dve, s_dm, n(0))
                    dve.tensor_reduce(deg[:, :], quad(adj_in[n.p(-1)][:, :]), AX.X, ALU.add).then_inc(s_deg, 1)
                if n.has(2):
                    dve.wait_ge(s_lin3ps, n(2))
                    dve.tensor_tensor(quad(lin3[:, :]), quad(ps_c[:, :]), row(b3_row), ALU.add).then_inc(s_lin3, 1)
                if n.has(3):
                    free(dve, s_store, n(4, 16))
                    apply(3, x4, res3, n, 3, s_x4)
            run(dve, step)

        @block.gpsimd
        def _(pool):
            def held():
                pool.nop(nofuse=True)

            def newton(i, n, lag):
                v, y_, a = var[i][:, :], rstd[i][:, :], nwt[i][:, :]
                pool.wait_ge(s_guess[i], n(lag))
                for k in range(NEWTON):
                    left = NSTEP[i] - 4 * k
                    if k:
                        pool.wait_ge(s_rstd[i], n(lag, NSTEP[i], left))
                    pool.tensor_tensor(a, y_, y_, ALU.mult).then_inc(s_rstd[i], 1)
                    pool.wait_ge(s_rstd[i], n(lag, NSTEP[i], left - 1))
                    pool.tensor_tensor(a, a, v, ALU.mult).then_inc(s_rstd[i], 1)
                    pool.wait_ge(s_rstd[i], n(lag, NSTEP[i], left - 2))
                    held()
                    pool.tensor_scalar(a, a, -0.5, 1.5, ALU.mult, ALU.add).then_inc(s_rstd[i], 1)
                    pool.wait_ge(s_rstd[i], n(lag, NSTEP[i], left - 3))
                    pool.tensor_tensor(y_, a, y_, ALU.mult).then_inc(s_rstd[i], 1)

            def shifts(i, n, lag):
                pool.wait_ge(s_rstd[i], n(lag, NSTEP[i]))
                pool.tensor_tensor(shift[i][:, :], neg_mean[i][:, :], rstd[i][:, 0:Q], ALU.mult).then_inc(s_shift[i], 1)

            pool.wait_ge(s_zero, 6)

            def step(n):
                if n.has(-1):
                    pool.wait_ge(s_xhi, n(-1))
                    pool.tensor_tensor(xT_lo[:, :], xT_in[n.p(-1)][:, :], xT_hi[:, :].bitcast(F32), ALU.subtract).then_inc(s_xlo, 1)
                if n.has(3):
                    pool.wait_ge(s_relu3, n(3))
                    pool.wait_ge(s_x3, n(3))
                    pool.tensor_tensor(res3[:, :], res3[:, :], x3[:, :], ALU.add).then_inc(s_res3, 1)
                if n.has(1):
                    pool.wait_ge(s_h1hi, n(1))
                    free(pool, s_conv2ps, n(2))
                    pool.tensor_tensor(h1_lo[:, :, PAD:PAD + P], quad(h1[:, :]), h1_hi[:, :, PAD:PAD + P].bitcast(F32),
                                       ALU.subtract).then_inc(s_h1lo, 1)
                    e = vl[:, :, 0:SE]
                    pool.wait_ge(s_emb, n(1))
                    pool.tensor_tensor(s_sq[:, :, :], e, e, ALU.mult).then_inc(s_sq_, 1)
                if n.has(2):
                    pool.wait_ge(s_gn, n(2))
                    free(pool, s_y, n(3))
                    pool.tensor_tensor(gd[:, :], x2T[n.p(2)][:, :], gn[:, :], ALU.subtract).then_inc(s_gd, 1)
                if n.has(1):
                    pool.tensor_tensor(vr_of(0, SE), e, e, ALU.add)
                    pool.wait_ge(s_sq_, n(1))
                    pool.tensor_tensor(s_sum_t[:, :], s_sq[:, :, 0], s_sq[:, :, 1], ALU.add).then_inc(s_sum, 1)
                    pool.wait_ge(s_sum, n(1))
                    pool.tensor_tensor(vl[:, :, 3], s_sum_t[:, :], s_sq[:, :, 2], ALU.add).then_inc(s_norm, 1)
                    pool.wait_ge(s_norm, n(1))
                    held()
                    pool.tensor_scalar(vr_of(4, 5), vl[:, :, 3:4], -1.0, None, ALU.mult).then_inc(s_v, 1)
                if n.has(0):
                    free(pool, s_x1, n(1))
                    shifts(0, n, 0)
                    pool.wait_ge(s_x1, n(0))
                    free(pool, s_res1, n(1))
                    pool.tensor_tensor(quad(x1_b[:, :]), quad(x1[:, :]), row(b1_row), ALU.add).then_inc(s_x1b, 1)
                if n.has(2):
                    free(pool, s_x3, n(3))
                    shifts(2, n, 2)
                if n.has(3):
                    newton(3, n, 3)
                if n.has(0):
                    free(pool, s_x2, n(1))
                    shifts(1, n, 0)
                if n.has(2):
                    pool.wait_ge(s_lin3, n(2))
                    pool.wait_ge(s_dmc, n(2))
                    free(pool, s_out3ps, n(3))
                    pool.tensor_tensor(quad(lin3_d[:, :]), quad(lin3[:, :]), per_graph(dm), ALU.mult).then_inc(s_lin3d, 1)
            run(pool, step)


def kernel(**inputs):
    import numpy as _np
    import concourse.bacc as _bacc
    from concourse import mybir as _mybir
    from concourse.bass_utils import run_bass_kernel_spmd as _run

    def grouped(a):
        a = _np.asarray(a).reshape(GROUPS, Q, P, P)
        return _np.ascontiguousarray(a.transpose(0, 2, 1, 3)).reshape(GROUPS * P, W)

    def rows(a):
        return _np.ascontiguousarray(_np.asarray(a).T)

    x, adj = _np.asarray(inputs["x"]), _np.asarray(inputs["adj"])
    conv2 = _np.asarray(inputs["L2_gnn_conv2_w"])
    arrays = {
        "x": grouped(x),
        "xT": grouped(x.transpose(0, 2, 1)),
        "adj": grouped(adj),
        "adjT": grouped(adj.transpose(0, 2, 1)),
        "mask": _np.asarray(inputs["nodemask"]).reshape(GROUPS, W),
        "w0": _np.asarray(inputs["L0_gnn_W"]),
        "w1": _np.asarray(inputs["L1_gnn_weight"]),
        "b1": _np.asarray(inputs["L1_gnn_bias"]).reshape(1, P),
        "conv1": rows(_np.asarray(inputs["L2_gnn_conv1_w"]).reshape(P, P)),
        "conv2": _np.ascontiguousarray(conv2.transpose(1, 2, 0)).reshape(P, TAPS * P),
        "bn": _np.ascontiguousarray(_np.stack([_np.asarray(inputs[f"L2_gnn_bn{i}_{v}"])
                                               for i in (1, 2) for v in "gbmv"], axis=1)),
        "wih": rows(inputs["L2_gnn_w_ih"]),
        "whh": rows(inputs["L2_gnn_w_hh"]),
        "bih": rows(_np.asarray(inputs["L2_gnn_b_ih"]).reshape(3, P)),
        "bhh": rows(_np.asarray(inputs["L2_gnn_b_hh"]).reshape(3, P)),
        "wmsg": rows(inputs["L2_gnn_w_msg"]),
        "wse": rows(inputs["L2_gnn_w_se"]),
        "bmsg": _np.asarray(inputs["L2_gnn_b_msg"]).reshape(1, P),
        "bse": _np.asarray(inputs["L2_gnn_b_se"]).reshape(1, SE),
        "w3": rows(inputs["L3_gnn_W"]),
        "b3": _np.asarray(inputs["L3_gnn_b"]).reshape(1, P),
        "eye": _np.eye(P, dtype=_np.float32),
    }
    nc = _bacc.Bacc("TRN2", target_bir_lowering=False, num_devices=1)
    args = [nc.dram_tensor(f"in_{k}", a.shape, _mybir.dt.from_np(a.dtype), kind="ExternalInput").ap()
            for k, a in arrays.items()]
    args.append(nc.dram_tensor("out_0", (GROUPS * P, W), _mybir.dt.float32, kind="ExternalOutput").ap())
    four_gnn_layers(nc, *args)
    r = _run(nc, [{f"in_{k}": a for k, a in arrays.items()}], core_ids=[0])
    out = r.results[0]["out_0"].reshape(GROUPS, P, Q, P)
    return _np.ascontiguousarray(out.transpose(0, 2, 1, 3)).reshape(128, P, P)
```

```python
from contextlib import ExitStack

import concourse.bass as bass
from concourse import mybir

F32 = mybir.dt.float32
F32R = mybir.dt.float32r
I32 = mybir.dt.int32
ALU = mybir.AluOpType
ACT = mybir.ActivationFunctionType
AX = mybir.AxisListType

P = 128
Q = 4
W = Q * P
GROUPS = 128 // Q
TAPS = 17
PAD = TAPS // 2
PHASE = P // 2
WIDE = PHASE + 2
PHW = PHASE + PAD + 2
H = W // 2
EVEN_TAPS, ODD_TAPS = (TAPS + 1) // 2, TAPS // 2
FILTERS = 2 * EVEN_TAPS + ODD_TAPS
LAST_LAG = 3
FIRST_STEADY = 4
END_STEADY = GROUPS - 2
EPS = 1e-5
MASKED = 1e30
MAGIC = float(0x5F3759DF)
NEWTON = 3
LOADS = 4
NSTEP = {0: 3 * NEWTON, 1: 3 * NEWTON, 2: 4 * NEWTON, 3: 4 * NEWTON}
VEC_STEPS = 2 + 3 * NEWTON + 8

U_W0, U_CONV1, U_CONV2 = 0, 1, 2
U_IH_CONV, U_IH_NMP, U_HH = U_CONV2 + TAPS, U_CONV2 + TAPS + 3, U_CONV2 + TAPS + 6
FIRST_UNITS = U_CONV2
U_SUM = U_HH + 3
UNITS = U_SUM + ODD_TAPS
GATE_R, GATE_Z, GATE_N = 0, 1, 2
SE = 3
DIST = SE + 2
VW = 32


def four_gnn_layers(nc, x_d, xT_d, adj_d, adjT_d, mask_d, w0_d, w1_d, b1_d, conv1_d, conv2_d,
                    bn_d, wih_d, whh_d, bih_d, bhh_d, wmsg_d, wse_d, bmsg_d, bse_d, w3_d, b3_d,
                    eye_d, out_d):
    ctx = ExitStack()
    with ctx:
        def sb(name, cols, dt=F32):
            return ctx.enter_context(nc.sbuf_tensor(name, [P, *cols], dt))

        def sem(name):
            return ctx.enter_context(nc.semaphore(name))

        staging = sb("staging", [UNITS * P])
        w_hi = sb("w_hi", [UNITS * P], F32R)
        w_lo = sb("w_lo", [UNITS * P], F32R)
        w1 = sb("w1", [P])
        w3 = sb("w3", [P])
        w_msg = sb("w_msg", [P + SE])
        w3c = sb("w3c", [P])
        centre = sb("centre", [P])
        eye = sb("eye", [P])
        b1_row = sb("b1_row", [P])
        b3_row = sb("b3_row", [P])
        bmsg_row = sb("bmsg_row", [P])
        bse_row = sb("bse_row", [SE])
        bn = sb("bn", [8])
        bih = sb("bih", [3])
        bhh = sb("bhh", [3])
        aff = sb("aff", [5])
        gate_b = sb("gate_b", [4])
        tmp = sb("tmp", [8])
        dm_all = sb("dm_all", [GROUPS * Q])
        dm = sb("dm", [Q])

        x_in = [sb(f"x_in{p}", [W]) for p in range(2)]
        xT_in = [sb(f"xT_in{p}", [W]) for p in range(2)]
        adj_in = [sb(f"adj_in{p}", [W]) for p in range(2)]
        adjT_in = [sb(f"adjT_in{p}", [W]) for p in range(2)]
        mask_in = [sb(f"mask_in{p}", [W], I32) for p in range(2)]
        xT_hi = sb("xT_hi", [W], F32R)
        xT_lo = sb("xT_lo", [W], F32R)
        mask_add = sb("mask_add", [W])
        deg = sb("deg", [Q])
        inter = sb("inter", [W])
        logit = sb("logit", [W])
        logit_min = sb("logit_min", [Q])
        prob = sb("prob", [W])
        prob_sum = sb("prob_sum", [Q])
        prob_inv = sb("prob_inv", [Q])
        probT = sb("probT", [W])
        res0 = sb("res0", [W])
        x1 = sb("x1", [W])
        aggT = sb("aggT", [W])
        x1_b = sb("x1_b", [W])
        res1 = sb("res1", [W])
        x2 = sb("x2", [W])
        x2T = [sb(f"x2T{p}", [W]) for p in range(2)]
        x2T_hi = [sb(f"x2T_hi{p}", [W], F32R) for p in range(2)]
        x2T_lo = [sb(f"x2T_lo{p}", [W], F32R) for p in range(2)]
        x2T_b = sb("x2T_b", [W])
        h1 = sb("h1", [W])
        h_hi = sb("h_hi", [3, Q, PHW], F32R)
        h_lo = sb("h_lo", [3, Q, PHW], F32R)
        h_sum = sb("h_sum", [H])
        msg_b = sb("msg_b", [W])
        msg = sb("msg", [W])
        left = sb("left", [Q, DIST])
        right = sb("right", [Q, DIST])
        vl = sb("vl", [Q, VW])
        vr = sb("vr", [Q * (P + VW)])
        s_sq = sb("s_square", [Q, SE])
        s_sum_t = sb("s_sum_t", [Q])
        vlT = sb("vlT", [P], F32R)
        vrT = sb("vrT", [W], F32R)
        near = sb("near", [W])
        near_adjT = sb("near_adjT", [W])
        nmp_hi = sb("nmp_hi", [W], F32R)
        nmp_lo = sb("nmp_lo", [W], F32R)
        conv_q = sb("conv_q", [Q, WIDE])
        conv = sb("conv", [W])
        conv_hi = sb("conv_hi", [W], F32R)
        conv_lo = sb("conv_lo", [W], F32R)
        gr = sb("gr", [W])
        gz = sb("gz", [W])
        gh = sb("gh", [W])
        gw = sb("gw", [W])
        gn = sb("gn", [W])
        gd = sb("gd", [W])
        y = sb("y", [W])
        x3 = sb("x3", [W])
        lin3 = sb("lin3", [W])
        bias3_d = sb("bias3_d", [W])
        scale3 = sb("scale3", [Q])
        lin3_d = sb("lin3_d", [W])
        res3 = sb("res3", [W])
        x4 = sb("x4", [W])
        adjT3 = [sb(f"adjT3{p}", [W]) for p in range(2)]
        stats = [sb(f"stats{i}", [Q, 6]) for i in range(4)]
        mv = [sb(f"mv{i}", [Q, 2]) for i in range(4)]
        var = [sb(f"var{i}", [2 * Q if i == 0 else Q]) for i in range(4)]
        rstd = [sb(f"rstd{i}", [2 * Q if i == 0 else Q]) for i in range(4)]
        nwt = [sb(f"nwt{i}", [2 * Q if i == 0 else Q]) for i in range(4)]
        neg_mean = [sb(f"neg_mean{i}", [Q]) for i in range(4)]
        shift = [sb(f"shift{i}", [Q]) for i in range(4)]

        def bank(name):
            return ctx.enter_context(nc.psum_tensor(name, [P, 512], F32))

        ps_a, ps_b, ps_c, ps_d = bank("ps_a"), bank("ps_b"), bank("ps_c"), bank("ps_d")
        ps_r, ps_z, ps_n, ps_h = bank("ps_r"), bank("ps_z"), bank("ps_n"), bank("ps_h")

        s_w = sem("s_w")
        s_wfirst, s_wsum = sem("s_wfirst"), sem("s_wsum")
        s_whi, s_wlo = sem("s_whi"), sem("s_wlo")
        s_centre, s_w3ps, s_w3c = sem("s_centre"), sem("s_w3ps"), sem("s_w3c")
        s_zero, s_const, s_vec = sem("s_zero"), sem("s_const"), sem("s_vec")
        s_loadT = [sem(f"s_loadT{p}") for p in range(2)]
        s_load = [sem(f"s_load{p}") for p in range(2)]
        s_adj3 = [sem(f"s_adj3{p}") for p in range(2)]
        s_store = sem("s_store")
        (s_xhi, s_xlo, s_mask, s_deg, s_interps, s_inter, s_scoreps, s_prod, s_logit, s_prob,
         s_probTps, s_probT, s_inv, s_out0ps, s_res0, s_x1, s_dm) = (sem(x) for x in (
            "s_xhi", "s_xlo", "s_mask", "s_deg", "s_interps", "s_inter", "s_scoreps", "s_prod",
            "s_logit", "s_prob", "s_probTps", "s_probT", "s_inv", "s_out0ps", "s_res0", "s_x1",
            "s_dm"))
        (s_aggps, s_agg, s_x1b, s_out1ps, s_res1, s_x2) = (sem(x) for x in (
            "s_aggps", "s_agg", "s_x1b", "s_out1ps", "s_res1", "s_x2"))
        (s_x2Tps, s_x2T, s_x2Thi, s_x2Tlo, s_x2Tb, s_conv1ps, s_h1, s_h1hi, s_h1lo, s_msgps, s_msgb,
         s_msg, s_emb, s_square, s_sum, s_v, s_vps, s_vlT, s_vrT, s_distps, s_near, s_nadj, s_nmpps,
         s_nmphi, s_nmplo, s_conv2ps, s_conv, s_convhi, s_convlo, s_hs, s_hshi, s_hslo, s_convqps,
         s_qs, s_z, s_zp) = (sem(x) for x in (
            "s_x2Tps", "s_x2T", "s_x2Thi", "s_x2Tlo", "s_x2Tb", "s_conv1ps", "s_h1", "s_h1hi",
            "s_h1lo", "s_msgps", "s_msgb", "s_msg", "s_emb", "s_square", "s_sum", "s_v", "s_vps",
            "s_vlT", "s_vrT", "s_distps", "s_near", "s_nadj", "s_nmpps", "s_nmphi", "s_nmplo",
            "s_conv2ps", "s_conv", "s_convhi", "s_convlo", "s_hs", "s_hshi", "s_hslo",
            "s_convqps", "s_qs", "s_z", "s_zp"))
        (s_ghps, s_gateps, s_gr, s_gh, s_gz, s_gw, s_gw2, s_gn, s_gd, s_ge, s_y) = (
            sem(x) for x in ("s_ghps", "s_gateps", "s_gr", "s_gh", "s_gz", "s_gw", "s_gw2",
                             "s_gn", "s_gd", "s_ge", "s_y"))
        (s_yTps, s_x3, s_bias3d, s_scale3, s_lin3ps, s_lin3, s_dmc, s_lin3d, s_out3ps, s_relu3,
         s_res3, s_x4) = (sem(x) for x in (
            "s_yTps", "s_x3", "s_bias3d", "s_scale3", "s_lin3ps", "s_lin3", "s_dmc", "s_lin3d",
            "s_out3ps", "s_relu3", "s_res3", "s_x4"))
        s_stats = [sem(f"s_stats{i}") for i in range(4)]
        s_mv = [sem(f"s_mv{i}") for i in range(4)]
        s_var = [sem(f"s_var{i}") for i in range(4)]
        s_guess = [sem(f"s_guess{i}") for i in range(4)]
        s_rstd = [sem(f"s_rstd{i}") for i in range(4)]
        s_shift = [sem(f"s_shift{i}") for i in range(4)]

        s_norm, s_vhi, s_vlo = sem("s_norm"), sem("s_vhi"), sem("s_vlo")

        def parts(blocks):
            return blocks[:, :, 0:3 * DIST].rearrange("p q (s c) -> p q s c", c=DIST).bitcast(F32R)

        def twice(tile):
            return tile[:, :, :].unsqueeze(2).broadcast_to((P, Q, 2, DIST))

        def col(tile, q):
            return tile[:, q * P:(q + 1) * P]

        def quad(ap):
            return ap.rearrange("p (q n) -> p q n", q=Q)

        def phases(tile):
            return tile.rearrange("p (c r) -> p r c", r=2)

        def phases_q(tile):
            return tile.rearrange("p (q c r) -> p r q c", q=Q, r=2)

        def row(tile, n=P):
            return tile[:, 0:n].unsqueeze(1).broadcast_to((P, Q, n))

        def per_graph(tile):
            return tile[:, 0:Q].unsqueeze(2).broadcast_to((P, Q, P))

        class Step:

            def __init__(self, eng, even, u, kept):
                self.eng, self.even, self.u, self.kept = eng, even, u, kept
                self.fixed = isinstance(even, int)

            def p(self, lag):
                return (self.u + lag) % 2

            def has(self, lag):
                return not self.fixed or 0 <= self.even + self.u - lag < GROUPS

            def __call__(self, lag, k=1, less=0):
                c = self.u - lag + 1
                if self.fixed:
                    return k * min(self.even + c, GROUPS) - less
                if k not in self.kept:
                    self.kept[k] = {}
                if k == 1:
                    if c not in self.kept[k]:
                        self.kept[k][c] = self.eng.snap(self.even + c)
                    return self.kept[k][c]
                if 0 not in self.kept[k]:
                    self.kept[k][0] = self.eng.snap(self.even * k)
                return self.kept[k][0] + (k * c - less)

            def halves(self, lag, k):
                c = (self.u - lag) // 2 + 1
                if self.fixed:
                    return k * (self.even // 2 + c)
                if ("h", k) not in self.kept:
                    self.kept["h", k] = self.eng.snap(self.even * (k // 2))
                return self.kept["h", k] + k * c

            def at(self, lag, unit):
                return (self.even + (self.u - lag)) * unit

        def free(eng, sema, value):
            if not isinstance(value, int) or value > 0:
                eng.wait_ge(sema, value)

        def run(eng, step, before={}):
            for t in range(-1, FIRST_STEADY):
                if t in before:
                    before[t]()
                step(Step(eng, t - t % 2, t % 2, {}))
            with eng.Fori(FIRST_STEADY // 2, END_STEADY // 2) as pair:
                kept, even = {}, pair * 2
                for u in range(2):
                    step(Step(eng, even, u, kept))
            for t in range(END_STEADY, GROUPS + LAST_LAG):
                step(Step(eng, t - t % 2, t % 2, {}))

        block = ctx.enter_context(nc.Block())

        @block.sync
        def _(sp):
            def load(g, p):
                rows = bass.ds(g * P, P)
                sp.dma_start(xT_in[p][:, :], xT_d[rows, :]).then_inc(s_load[p], 16)
                sp.dma_start(adj_in[p][:, :], adj_d[rows, :]).then_inc(s_load[p], 16)
                sp.dma_start(mask_in[p][:, :], mask_d[bass.ds(g, 1), :].broadcast_to((P, W))).then_inc(s_load[p], 16)
                sp.dma_start(x_in[p][:, :], x_d[rows, :]).then_inc(s_load[p], 16)

            def load_adjT(g, p):
                sp.dma_start(adjT_in[p][:, :], adjT_d[bass.ds(g * P, P), :]).then_inc(s_loadT[p], 16)

            for src, u0 in [(w0_d, U_W0), (conv1_d, U_CONV1)]:
                sp.dma_start(staging[:, u0 * P:(u0 + 1) * P], src).then_inc(s_wfirst, 16)
            load(0, 0)
            units = [(conv2_d, U_CONV2, TAPS),
                     (wih_d[0:P, :], U_IH_CONV, 3), (wih_d[P:2 * P, :], U_IH_NMP, 3), (whh_d, U_HH, 3)]
            for src, u0, k in units:
                sp.dma_start(staging[:, u0 * P:(u0 + k) * P], src).then_inc(s_w, 16)
            for dst, src in [(w1[:, :], w1_d), (w3[:, :], w3_d), (w_msg[:, 0:P], wmsg_d),
                             (w_msg[:, P:P + SE], wse_d), (eye[:, :], eye_d),
                             (b1_row[:, :], b1_d.broadcast_to((P, P))),
                             (b3_row[:, :], b3_d.broadcast_to((P, P))),
                             (bmsg_row[:, :], bmsg_d.broadcast_to((P, P))),
                             (bse_row[:, :], bse_d.broadcast_to((P, SE))),
                             (bn[:, :], bn_d), (bih[:, :], bih_d), (bhh[:, :], bhh_d)]:
                sp.dma_start(dst, src).then_inc(s_const, 16)
            load(1, 1)
            load_adjT(0, 0)

            def held():
                sp.nop(nofuse=True)

            def step(n):
                if n.has(1):
                    free(sp, s_out3ps, n(3))
                    held()
                    sp.wait_ge(s_aggps, n(1))
                    sp.dma_start(adjT3[n.p(1)][:, :], adjT_in[n.p(1)][:, :]).then_inc(s_adj3[n.p(1)], 16)
                if n.has(0) and n.has(-2):
                    sp.wait_ge(s_res0, n(0))
                    held()
                    load(n.even + (n.u + 2), n.p(0))
                if n.has(-1) and n.has(0):
                    if n.has(1):
                        sp.wait_ge(s_nadj, n(1))
                        held()
                        sp.wait_ge(s_adj3[n.p(1)], n.halves(1, 16))
                        held()
                    load_adjT(n.even + (n.u + 1), n.p(-1))
                if n.has(3):
                    sp.wait_ge(s_x4, n(3))
                    held()
                    sp.dma_start(out_d[bass.ds(n.at(3, P), P), :], x4[:, :]).then_inc(s_store, 16)
            run(sp, step)
            sp.wait_ge(s_store, 16 * GROUPS)

        @block.tensor
        def _(pe):
            def split_product(ps, unit, hi, lo, start, stop):
                wh, wl = w_hi[:, unit * P:(unit + 1) * P], w_lo[:, unit * P:(unit + 1) * P]
                pe.matmul(ps, wh, hi, start=start, stop=False)
                pe.matmul(ps, wh, lo, start=False, stop=False)
                return pe.matmul(ps, wl, hi, start=False, stop=stop)

            def taps(n, a, b):
                if not n.has(1):
                    return
                for k in range(a, b):
                    if k < EVEN_TAPS:
                        j, ps, unit, part, width, count = k, ps_n[:, H:W], U_CONV2 + 2 * k, 1, PHASE, EVEN_TAPS
                    elif k < EVEN_TAPS + ODD_TAPS:
                        j, width, count = k - EVEN_TAPS, WIDE, ODD_TAPS
                        ps, unit, part = ps_r[:, 0:Q * width], U_CONV2 + 2 * j + 1, 0
                    else:
                        j, ps, part, width, count = k - EVEN_TAPS - ODD_TAPS, ps_n[:, 0:H], 2, PHASE, EVEN_TAPS
                        unit = U_SUM + j if j < ODD_TAPS else U_CONV2 + 2 * j
                    if k == 0 and n.fixed:
                        pe.wait_ge(s_whi, 2)
                        pe.wait_ge(s_wlo, 2)
                    if k == 0:
                        pe.wait_ge(s_h1hi, n(1))
                        pe.wait_ge(s_h1lo, n(1))
                        free(pe, s_zp, n(2))
                    if k == EVEN_TAPS:
                        free(pe, s_gr, n(2))
                    if k == EVEN_TAPS + ODD_TAPS:
                        pe.wait_ge(s_hshi, n(1))
                        pe.wait_ge(s_hslo, n(1))
                    mm = split_product(ps, unit, h_hi[:, part, :, j:j + width],
                                       h_lo[:, part, :, j:j + width], j == 0, j == count - 1)
                    if k == EVEN_TAPS + ODD_TAPS - 1:
                        mm.then_inc(s_convqps, 1)
                    if k == FILTERS - 1:
                        mm.then_inc(s_conv2ps, 1)

            def centred_weights():
                pe.wait_ge(s_centre, 1)
                pe.matmul(ps_c[:, 0:P], centre[:, :], w3[:, :], start=True, stop=True).then_inc(s_w3ps, 1)

            pe.wait_ge(s_whi, 1)
            pe.wait_ge(s_wlo, 1)

            def step(n):
                if n.has(0):
                    pe.wait_ge(s_prob, n(0))
                    for q in range(Q):
                        mm = pe.transpose(col(ps_b, q), col(prob, q), eye[:, :])
                    mm.then_inc(s_probTps, 1)
                if n.has(2):
                    xh, xl = x2T_hi[n.p(2)][:, :], x2T_lo[n.p(2)][:, :]
                    pe.wait_ge(s_qs, n(2))
                    free(pe, s_gz, n(3))
                    pe.wait_ge(s_vrT, n(2))
                    split_product(ps_r[:, :], U_HH + GATE_R, xh, xl, True, False)
                    split_product(ps_z[:, :], U_HH + GATE_Z, xh, xl, True, False)
                    split_product(ps_h[:, :], U_HH + GATE_N, xh, xl, True, True).then_inc(s_ghps, 1)
                if n.has(1):
                    pe.wait_ge(s_x2, n(1))
                    free(pe, s_nmphi, n(2))
                    free(pe, s_nmplo, n(2))
                    for q in range(Q):
                        mm = pe.transpose(col(ps_d, q), col(x2, q), eye[:, :])
                    mm.then_inc(s_x2Tps, 1)
                if n.has(3):
                    pe.wait_ge(s_lin3d, n(3))
                    pe.wait_ge(s_adj3[n.p(3)], n.halves(3, 16))
                    for q in range(Q):
                        mm = pe.matmul(col(ps_c, q), col(adjT3[n.p(3)], q), col(lin3_d, q), start=True, stop=True)
                    mm.then_inc(s_out3ps, 1)
                if n.has(0):
                    pe.wait_ge(s_probT, n(0))
                    free(pe, s_res1, n(1))
                    for q in range(Q):
                        mm = pe.matmul(col(ps_a, q), col(probT, q), col(x_in[n.p(0)], q), start=True, stop=True)
                    mm.then_inc(s_out0ps, 1)
                if n.has(2):
                    pe.wait_ge(s_nmplo, n(2))
                    split_product(ps_r[:, :], U_IH_NMP + GATE_R, nmp_hi[:, :], nmp_lo[:, :], False, False)
                    split_product(ps_z[:, :], U_IH_NMP + GATE_Z, nmp_hi[:, :], nmp_lo[:, :], False, False)
                if n.has(1):
                    pe.wait_ge(s_x2Tb, n(1))
                    pe.wait_ge(s_x2Tlo, n(1))
                    split_product(ps_d[:, :], U_CONV1, x2T_hi[n.p(1)][:, :], x2T_lo[n.p(1)][:, :],
                                  True, True).then_inc(s_conv1ps, 1)
                if n.has(2):
                    pe.wait_ge(s_convlo, n(2))
                    split_product(ps_r[:, :], U_IH_CONV + GATE_R, conv_hi[:, :], conv_lo[:, :], False, True).then_inc(s_gateps, 1)
                    pe.wait_ge(s_gh, n(2))
                    split_product(ps_h[:, :], U_IH_NMP + GATE_N, nmp_hi[:, :], nmp_lo[:, :], True, False)
                    split_product(ps_h[:, :], U_IH_CONV + GATE_N, conv_hi[:, :], conv_lo[:, :], False, True).then_inc(s_gateps, 1)
                if n.has(1):
                    pe.wait_ge(s_res0, n(0))
                    pe.wait_ge(s_h1, n(1))
                    for q in range(Q):
                        dst = (ps_a if q < 2 else ps_d)[:, (q % 2) * (P + SE):(q % 2 + 1) * (P + SE)]
                        mm = pe.matmul(dst, col(x2T[n.p(1)], q), w_msg[:, :], start=True, stop=True)
                    mm.then_inc(s_msgps, 1)
                if n.has(2):
                    split_product(ps_z[:, :], U_IH_CONV + GATE_Z, conv_hi[:, :], conv_lo[:, :], False, True).then_inc(s_gateps, 1)
                if n.has(-1):
                    pe.wait_ge(s_xhi, n(-1))
                    pe.wait_ge(s_xlo, n(-1))
                    free(pe, s_probT, n(0))
                    split_product(ps_b[:, :], U_W0, xT_hi[:, :], xT_lo[:, :], True, True).then_inc(s_interps, 1)
                taps(n, 0, 6)
                if n.has(-1):
                    pe.wait_ge(s_inter, n(-1))
                    for q in range(Q):
                        mm = pe.matmul(col(ps_b, q), col(inter, q), col(xT_in[n.p(-1)], q), start=True, stop=True)
                    mm.then_inc(s_scoreps, 1)
                taps(n, 6, 9)
                if n.has(2):
                    pe.wait_ge(s_y, n(2))
                    free(pe, s_relu3, n(3))
                    for q in range(Q):
                        mm = pe.transpose(col(ps_c, q), col(y, q), eye[:, :])
                    mm.then_inc(s_yTps, 1)
                taps(n, 9, 10)
                if n.has(0):
                    pe.wait_ge(s_x1, n(0))
                    free(pe, s_msgb, n(1))
                    pe.wait_ge(s_loadT[n.p(0)], n.halves(0, 16))
                    for q in range(Q):
                        mm = pe.matmul(col(ps_a, q), col(x1, q),
                                       col(adjT_in[n.p(0)], q), start=True, stop=True)
                    mm.then_inc(s_aggps, 1)
                taps(n, 10, 11)
                if n.has(1):
                    pe.wait_ge(s_vlo, n(1))
                    pe.wait_ge(s_msgb, n(1))
                    free(pe, s_gw2, n(2))
                    pe.transpose(ps_d[:, 0:P], vl[:, :, :].rearrange("p q c -> p (q c)"), eye[:, :])
                    for q in range(Q):
                        mm = pe.transpose(col(ps_h, q), vr[:, q * P:(q + 1) * P], eye[:, :])
                    mm.then_inc(s_vps, 1)
                taps(n, 11, 12)
                if n.has(0):
                    pe.wait_ge(s_agg, n(0))
                    for q in range(Q):
                        mm = pe.matmul(col(ps_a, q), col(aggT, q), w1[:, :], start=True, stop=True)
                    mm.then_inc(s_out1ps, 1)
                taps(n, 12, 14)
                if n.has(1):
                    pe.wait_ge(s_vrT, n(1))
                    pe.matmul(ps_d[:, :], vlT[:, :], vrT[:, :], start=True, stop=True).then_inc(s_distps, 1)
                taps(n, 14, 24)
                if n.has(1):
                    pe.wait_ge(s_nadj, n(1))
                    pe.wait_ge(s_msg, n(1))
                    for q in range(Q):
                        mm = pe.matmul(col(ps_d, q), col(msg, q), col(near_adjT, q), start=True, stop=True)
                    mm.then_inc(s_nmpps, 1)
                taps(n, 24, FILTERS)
                if n.has(2):
                    pe.wait_ge(s_x3, n(2))
                    for q in range(Q):
                        mm = pe.matmul(col(ps_c, q), col(y, q), w3c[:, :], start=True, stop=True)
                    mm.then_inc(s_lin3ps, 1)
            def constants():
                pe.wait_ge(s_const, 16 * 12)

            def centred_weights_read():
                pe.wait_ge(s_w3c, 1)

            run(pe, step, {0: constants, 1: centred_weights, 2: centred_weights_read})

        @block.scalar
        def _(act):
            def rest_of_weights():
                act.wait_ge(s_w, 16 * 4)
                act.wait_ge(s_wsum, 1)
                act.copy(w_hi[:, FIRST_UNITS * P:], staging[:, FIRST_UNITS * P:]).then_inc(s_whi, 1)

            act.wait_ge(s_wfirst, 16 * 2)
            act.copy(w_hi[:, 0:FIRST_UNITS * P], staging[:, 0:FIRST_UNITS * P]).then_inc(s_whi, 1)

            def apply(i, out, src, n, lag, done):
                act.wait_ge(s_shift[i], n(lag))
                for q in range(Q):
                    ins = act.activation(col(out, q), col(src, q), ACT.Identity, bias=shift[i][:, q:q + 1],
                                         scale=rstd[i][:, q:q + 1])
                ins.then_inc(done, 1)

            def step(n):
                if n.has(0):
                    act.wait_ge(s_probTps, n(0))
                    free(act, s_out0ps, n(1))
                    act.copy(probT[:, :], ps_b[:, :]).then_inc(s_probT, 1)
                if n.has(1):
                    act.wait_ge(s_x2Tps, n(1))
                    free(act, s_y, n(3))
                    act.copy(x2T[n.p(1)][:, :], ps_d[:, :]).then_inc(s_x2T, 1)
                    free(act, s_ghps, n(3))
                    act.copy(x2T_hi[n.p(1)][:, :], ps_d[:, :]).then_inc(s_x2Thi, 1)
                if n.has(2):
                    act.wait_ge(s_conv, n(2))
                    free(act, s_gateps, n(3, 3))
                    act.activation(phases(conv_hi[:, :]), conv[:, :].rearrange("p (r c) -> p r c", r=2),
                                   ACT.Relu).then_inc(s_convhi, 1)
                if n.has(1):
                    free(act, s_z, n(2))
                    act.activation(x2T_b[:, :].rearrange("p (r c) -> p r c", r=2), phases(ps_d[:, :]),
                                   ACT.Identity, bias=aff[:, 3:4]).then_inc(s_x2Tb, 1)
                if n.has(-1):
                    act.wait_ge(s_load[n.p(-1)], n.halves(-1, 16 * LOADS))
                    free(act, s_interps, n(0))
                    act.copy(xT_hi[:, :], xT_in[n.p(-1)][:, :]).then_inc(s_xhi, 1)
                if n.has(2):
                    act.wait_ge(s_ghps, n(2))
                    free(act, s_gw, n(3))
                    act.activation(gh[:, :], ps_h[:, :], ACT.Identity, bias=gate_b[:, 2:3], scale=0.5).then_inc(s_gh, 1)
                if n.has(1):
                    act.wait_ge(s_conv1ps, n(1))
                    free(act, s_h1lo, n(2))
                    free(act, s_hs, n(2))
                    act.activation(h1[:, :], ps_d[:, :], ACT.Relu, bias=aff[:, 2:3], scale=aff[:, 0:1]).then_inc(s_h1, 1)
                if n.has(2):
                    act.wait_ge(s_gateps, n(2, 3, 2))
                    free(act, s_gw, n(3))
                    act.activation(gr[:, :], ps_r[:, :], ACT.Tanh, bias=gate_b[:, 0:1], scale=0.5).then_inc(s_gr, 1)
                if n.has(1):
                    act.wait_ge(s_h1, n(1))
                    free(act, s_conv2ps, n(2))
                    act.copy(h_hi[:, 0:2, :, PAD // 2:PAD // 2 + PHASE], phases_q(h1[:, :])).then_inc(s_h1hi, 1)
                if n.has(2):
                    act.wait_ge(s_gw2, n(2))
                    free(act, s_gd, n(3))
                    act.activation(gn[:, :], gw[:, :], ACT.Tanh, bias=gate_b[:, 3:4]).then_inc(s_gn, 1)
                    act.wait_ge(s_gateps, n(2, 3))
                    free(act, s_ge, n(3))
                    act.activation(gz[:, :], ps_z[:, :], ACT.Tanh, bias=gate_b[:, 1:2], scale=0.5).then_inc(s_gz, 1)
                if n.has(1):
                    act.wait_ge(s_hs, n(1))
                    free(act, s_conv2ps, n(2))
                    act.copy(h_hi[:, 2, :, PAD // 2:PAD // 2 + PHASE],
                             h_sum[:, :].rearrange("p (q c) -> p q c", q=Q)).then_inc(s_hshi, 1)
                if n.has(-1):
                    act.wait_ge(s_interps, n(-1))
                    free(act, s_scoreps, n(0))
                    act.mul(inter[:, :], ps_b[:, :], -1.0).then_inc(s_inter, 1)
                if n.has(0):
                    free(act, s_aggps, n(1))
                    free(act, s_x1b, n(1))
                    apply(0, x1, res0, n, 0, s_x1)
                    act.wait_ge(s_aggps, n(0))
                    free(act, s_out1ps, n(1))
                    act.copy(aggT[:, :], ps_a[:, :]).then_inc(s_agg, 1)
                if n.has(1):
                    act.wait_ge(s_vps, n(1))
                    free(act, s_distps, n(2))
                    act.copy(vlT[:, :], ps_d[:, 0:P]).then_inc(s_vlT, 1)
                    act.copy(vrT[:, :], ps_h[:, :]).then_inc(s_vrT, 1)
                    act.wait_ge(s_distps, n(1))
                    free(act, s_nadj, n(2))
                    act.activation(near[:, :], ps_d[:, :], ACT.Exp).then_inc(s_near, 1)
                    act.wait_ge(s_msgb, n(1))
                    free(act, s_nmpps, n(2))
                    act.activation(msg[:, :], msg_b[:, :], ACT.Relu).then_inc(s_msg, 1)
                    act.wait_ge(s_convqps, n(1))
                    free(act, s_conv, n(2))
                    act.activation(conv_q[:, :, :].rearrange("p q c -> p (q c)"), ps_r[:, 0:Q * WIDE],
                                   ACT.Identity, scale=aff[:, 1:2]).then_inc(s_qs, 1)
                if n.has(-1):
                    act.wait_ge(s_logit, n(-1))
                    free(act, s_probTps, n(0))
                    free(act, s_inv, n(0))
                    for q in range(Q):
                        ins = act.activation(col(prob, q), col(logit, q), ACT.Exp, bias=logit_min[:, q:q + 1],
                                             scale=-1.0, accum_out=prob_sum[:, q:q + 1])
                    ins.then_inc(s_prob, 1)
                if n.has(2):
                    free(act, s_res3, n(3))
                    apply(2, x3, ps_c, n, 2, s_x3)
                if n.has(1):
                    act.wait_ge(s_nmpps, n(1))
                    free(act, s_gateps, n(2, 3))
                    act.copy(nmp_hi[:, :], ps_d[:, :]).then_inc(s_nmphi, 1)
                if n.has(0):
                    free(act, s_x2Tps, n(1))
                    apply(1, x2, res1, n, 0, s_x2)
                if n.has(3):
                    free(act, s_store, n(4, 16))
                    apply(3, x4, res3, n, 3, s_x4)
            def biases():
                act.wait_ge(s_vec, VEC_STEPS)

            run(act, step, {0: rest_of_weights, 1: biases})

        @block.vector
        def _(dve):
            def held():
                dve.nop(nofuse=True)

            def low_parts(a, b, count):
                dve.wait_ge(s_whi, count)
                part = slice(a * P, b * P)
                dve.tensor_tensor(w_lo[:, part], staging[:, part], w_hi[:, part].bitcast(F32), ALU.subtract).then_inc(s_wlo, 1)

            low_parts(0, FIRST_UNITS, 1)

            for tile in (h_hi, h_lo):
                dve.memset(tile[:, :, :, :].bitcast(F32), 0.0).then_inc(s_zero, 1)
            dve.memset(vl[:, :, :], 0.0).then_inc(s_zero, 1)
            dve.memset(vr[:, :], 0.0).then_inc(s_zero, 1)
            dve.memset(left[:, :, DIST - 1:DIST], -1.0).then_inc(s_zero, 1)
            dve.memset(right[:, :, SE:SE + 1], 1.0).then_inc(s_zero, 1)

            def weight_sums():
                dve.wait_ge(s_const, 16 * 12)
                dve.tensor_scalar(centre[:, :], eye[:, :], -1.0 / P, None, ALU.add).then_inc(s_centre, 1)

                dve.wait_ge(s_w, 16 * 4)
                taps_ = staging[:, U_CONV2 * P:(U_CONV2 + 2 * ODD_TAPS) * P].rearrange("p (j s c) -> p s j c", s=2, c=P)
                dve.tensor_tensor(staging[:, U_SUM * P:UNITS * P].rearrange("p (j c) -> p j c", c=P),
                                  taps_[:, 0], taps_[:, 1], ALU.add).then_inc(s_wsum, 1)

            def affine_forms():
                vec = [0]

                def chain(ins):
                    ins.then_inc(s_vec, 1)
                    vec[0] += 1
                    dve.wait_ge(s_vec, vec[0])

                two = lambda tile, a: tile[:, a:a + 5:4]
                dve.wait_ge(s_const, 16 * 12)
                v, g, a = tmp[:, 0:2], tmp[:, 2:4], tmp[:, 4:6]
                chain(dve.tensor_scalar(v, two(bn, 3), EPS, None, ALU.add))
                chain(dve.tensor_scalar(g.bitcast(I32), v.bitcast(I32), -0.5, MAGIC, ALU.mult, ALU.add))
                for _ in range(NEWTON):
                    chain(dve.scalar_tensor_tensor(out=a, in0=g, scalar=-0.5, in1=g, op0=ALU.mult, op1=ALU.mult))
                    chain(dve.tensor_tensor(a, a, v, ALU.mult))
                    chain(dve.scalar_tensor_tensor(out=g, in0=a, scalar=1.5, in1=g, op0=ALU.add, op1=ALU.mult))
                chain(dve.tensor_tensor(aff[:, 0:2], two(bn, 0), g, ALU.mult))
                chain(dve.tensor_tensor(a, two(bn, 2), aff[:, 0:2], ALU.mult))
                chain(dve.tensor_tensor(aff[:, 2:4], two(bn, 1), a, ALU.subtract))
                chain(dve.tensor_tensor(a, bih[:, 0:2], bhh[:, 0:2], ALU.add))
                chain(dve.tensor_scalar(gate_b[:, 0:2], a, 0.5, None, ALU.mult))
                chain(dve.tensor_scalar(gate_b[:, 2:3], bhh[:, 2:3], 0.5, None, ALU.mult))
                chain(dve.tensor_copy(gate_b[:, 3:4], bih[:, 2:3]))
                chain(dve.tensor_scalar(aff[:, 4:5], aff[:, 1:2], -1.0, None, ALU.mult))
                assert vec[0] == VEC_STEPS

            def rest_of_weights():
                dve.wait_ge(s_w3ps, 1)
                dve.tensor_copy(w3c[:, :], ps_c[:, 0:P]).then_inc(s_w3c, 1)
                low_parts(FIRST_UNITS, UNITS, 2)

            def look(i, src, n, lag):
                for q in range(Q):
                    ins = dve.bn_stats(stats[i][:, q, :], col(src, q))
                ins.then_inc(s_stats[i], 1)

            def moments(i, n, lag):
                dve.wait_ge(s_stats[i], n(lag))
                held()
                for q in range(Q):
                    ins = dve.bn_aggr(mv[i][:, q, :], stats[i][:, q, :])
                ins.then_inc(s_mv[i], 1)

            def spread(i, n, lag):
                dve.wait_ge(s_mv[i], n(lag))
                eps = 4 * EPS if i == 2 else EPS
                dve.tensor_scalar(neg_mean[i][:, :], mv[i][:, :, 0], -1.0, None, ALU.mult)
                dve.tensor_scalar(var[i][:, 0:Q], mv[i][:, :, 1], eps, None, ALU.add).then_inc(s_var[i], 1)

            def guess(i, n, lag):
                dve.wait_ge(s_var[i], n(lag))
                dve.tensor_scalar(rstd[i][:, :].bitcast(I32), var[i][:, :].bitcast(I32), -0.5, MAGIC,
                                  ALU.mult, ALU.add).then_inc(s_guess[i], 1)

            def newton(i, n, lag, first=0, last=NEWTON):
                v, y_, a = var[i][:, :], rstd[i][:, :], nwt[i][:, :]
                for k in range(first, last):
                    left = NSTEP[i] - 3 * k
                    if k == 0:
                        dve.wait_ge(s_guess[i], n(lag))
                    else:
                        dve.wait_ge(s_rstd[i], n(lag, NSTEP[i], left))
                    dve.scalar_tensor_tensor(out=a, in0=y_, scalar=-0.5, in1=y_, op0=ALU.mult,
                                             op1=ALU.mult).then_inc(s_rstd[i], 1)
                    dve.wait_ge(s_rstd[i], n(lag, NSTEP[i], left - 1))
                    dve.tensor_tensor(a, a, v, ALU.mult).then_inc(s_rstd[i], 1)
                    dve.wait_ge(s_rstd[i], n(lag, NSTEP[i], left - 2))
                    dve.scalar_tensor_tensor(out=y_, in0=a, scalar=1.5, in1=y_, op0=ALU.add,
                                             op1=ALU.mult).then_inc(s_rstd[i], 1)

            def message_part(h):
                return (ps_a, ps_d)[h][:, 0:2 * (P + SE)].rearrange("p (q c) -> p q c", q=2)

            def step(n):
                if n.has(0):
                    dve.wait_ge(s_prob, n(0))
                    dve.reciprocal(prob_inv[:, :], prob_sum[:, :]).then_inc(s_inv, 1)
                if n.has(2):
                    dve.wait_ge(s_conv2ps, n(2))
                    dve.wait_ge(s_x2Tb, n(2))
                    free(dve, s_convhi, n(3))
                    free(dve, s_convlo, n(3))
                    dve.scalar_tensor_tensor(out=conv[:, :], in0=ps_n[:, :], scalar=aff[:, 1:2], in1=x2T_b[:, :],
                                             op0=ALU.mult, op1=ALU.add).then_inc(s_z, 1)
                if n.has(-1):
                    dve.wait_ge(s_load[n.p(-1)], n.halves(-1, 16 * LOADS))
                    free(dve, s_logit, n(0))
                    dve.tensor_scalar(mask_add[:, :], mask_in[n.p(-1)][:, :], 0, MASKED, ALU.is_equal, ALU.mult).then_inc(s_mask, 1)
                if n.has(2):
                    dve.wait_ge(s_z, n(2))
                    dve.scalar_tensor_tensor(out=conv[:, 0:H], in0=ps_n[:, H:W], scalar=aff[:, 4:5], in1=conv[:, 0:H],
                                             op0=ALU.mult, op1=ALU.add).then_inc(s_zp, 1)
                if n.has(3):
                    dve.wait_ge(s_out3ps, n(3))
                    dve.wait_ge(s_dmc, n(3))
                    free(dve, s_x4, n(4))
                    dve.scalar_tensor_tensor(out=quad(res3[:, :]), in0=quad(ps_c[:, :]), scalar=0.0, in1=per_graph(dm),
                                             op0=ALU.max, op1=ALU.mult).then_inc(s_relu3, 1)
                if n.has(1):
                    dve.wait_ge(s_x2Thi, n(1))
                    free(dve, s_ghps, n(3))
                    dve.tensor_tensor(x2T_lo[n.p(1)][:, :], x2T[n.p(1)][:, :], x2T_hi[n.p(1)][:, :].bitcast(F32),
                                      ALU.subtract).then_inc(s_x2Tlo, 1)
                if n.has(2):
                    dve.wait_ge(s_convhi, n(2))
                    free(dve, s_gateps, n(3, 3))
                    dve.scalar_tensor_tensor(out=phases(conv_lo[:, :]), in0=conv[:, :].rearrange("p (r c) -> p r c", r=2),
                                             scalar=0.0, in1=phases(conv_hi[:, :].bitcast(F32)),
                                             op0=ALU.max, op1=ALU.subtract).then_inc(s_convlo, 1)
                if n.has(0):
                    dve.wait_ge(s_out0ps, n(0))
                    dve.wait_ge(s_inv, n(0))
                    free(dve, s_x1, n(1))
                    for q in range(Q):
                        ins = dve.scalar_tensor_tensor(out=col(res0, q), in0=col(ps_a, q), scalar=prob_inv[:, q:q + 1],
                                                       in1=col(x_in[n.p(0)], q), op0=ALU.mult, op1=ALU.add)
                    ins.then_inc(s_res0, 1)
                if n.has(2):
                    free(dve, s_lin3d, n(3))
                    free(dve, s_relu3, n(3))
                    dve.tensor_copy(dm[:, :], dm_all[:, bass.ds(n.at(2, Q), Q)]).then_inc(s_dmc, 1)
                if n.has(0):
                    dve.wait_ge(s_deg, n(0))
                    dve.scalar_tensor_tensor(out=var[0][:, Q:2 * Q], in0=deg[:, :], scalar=0.0, in1=deg[:, :],
                                             op0=ALU.is_equal, op1=ALU.add)
                    dve.wait_ge(s_res0, n(0))
                    look(0, res0, n, 0)
                if n.has(1):
                    dve.wait_ge(s_h1, n(1))
                    free(dve, s_hshi, n(2))
                    free(dve, s_hslo, n(2))
                    dve.tensor_tensor(h_sum[:, :], phases(h1[:, :])[:, 0, :], phases(h1[:, :])[:, 1, :],
                                      ALU.add).then_inc(s_hs, 1)
                if n.has(0):
                    moments(0, n, 0)
                if n.has(2):
                    dve.wait_ge(s_gr, n(2))
                    dve.wait_ge(s_gh, n(2))
                    free(dve, s_gn, n(3))
                    dve.scalar_tensor_tensor(out=gw[:, :], in0=gr[:, :], scalar=1.0, in1=gh[:, :],
                                             op0=ALU.add, op1=ALU.mult).then_inc(s_gw, 1)
                if n.has(0):
                    spread(0, n, 0)
                if n.has(2):
                    dve.wait_ge(s_gateps, n(2, 3, 1))
                    dve.wait_ge(s_gw, n(2))
                    dve.tensor_tensor(gw[:, :], gw[:, :], ps_h[:, :], ALU.add).then_inc(s_gw2, 1)
                if n.has(0):
                    guess(0, n, 0)
                if n.has(1):
                    dve.wait_ge(s_msgps, n(1))
                    free(dve, s_vlo, n(2))
                    for h in range(2):
                        ins = dve.tensor_tensor(right[:, 2 * h:2 * h + 2, 0:SE], message_part(h)[:, :, P:P + SE],
                                                bse_row[:, :].unsqueeze(1).broadcast_to((P, 2, SE)), ALU.add)
                    ins.then_inc(s_emb, 1)
                if n.has(0):
                    newton(0, n, 0, 0, 3)
                if n.has(1):
                    free(dve, s_msg, n(2))
                    for h in range(2):
                        ins = dve.tensor_tensor(quad(msg_b[:, :])[:, 2 * h:2 * h + 2, :], message_part(h)[:, :, 0:P],
                                                bmsg_row[:, :].unsqueeze(1).broadcast_to((P, 2, P)), ALU.add)
                    ins.then_inc(s_msgb, 1)
                if n.has(2):
                    dve.wait_ge(s_gd, n(2))
                    dve.wait_ge(s_gz, n(2))
                    dve.scalar_tensor_tensor(out=gd[:, :], in0=gz[:, :], scalar=-1.0, in1=gd[:, :],
                                             op0=ALU.add, op1=ALU.mult).then_inc(s_ge, 1)
                if n.has(0):
                    dve.wait_ge(s_rstd[0], n(0, NSTEP[0]))
                    dve.scalar_tensor_tensor(out=dm_all[:, bass.ds(n.at(0, Q), Q)], in0=deg[:, :], scalar=0.0,
                                             in1=rstd[0][:, Q:2 * Q], op0=ALU.not_equal, op1=ALU.mult).then_inc(s_dm, 1)
                if n.has(2):
                    dve.wait_ge(s_ge, n(2))
                    free(dve, s_lin3ps, n(3))
                    dve.scalar_tensor_tensor(out=y[:, :], in0=x2T[n.p(2)][:, :], scalar=4.0, in1=gd[:, :],
                                             op0=ALU.mult, op1=ALU.add).then_inc(s_y, 1)
                if n.has(3):
                    dve.wait_ge(s_res3, n(3))
                    look(3, res3, n, 3)
                if n.has(2):
                    dve.wait_ge(s_yTps, n(2))
                    held()
                    look(2, ps_c, n, 2)
                    moments(2, n, 2)
                if n.has(3):
                    moments(3, n, 3)
                if n.has(2):
                    spread(2, n, 2)
                if n.has(3):
                    free(dve, s_x4, n(4))
                    spread(3, n, 3)
                if n.has(2):
                    guess(2, n, 2)
                if n.has(-1):
                    dve.wait_ge(s_scoreps, n(-1))
                    free(dve, s_prob, n(0))
                    dve.tensor_tensor(logit[:, :], ps_b[:, :], adj_in[n.p(-1)][:, :], ALU.mult).then_inc(s_prod, 1)
                    dve.wait_ge(s_prod, n(-1))
                    dve.wait_ge(s_mask, n(-1))
                    held()
                    for q in range(Q):
                        ins = dve.tensor_tensor_reduce(col(logit, q), col(logit, q), col(mask_add, q), 1.0, MASKED * 2,
                                                       ALU.add, ALU.min, logit_min[:, q:q + 1])
                    ins.then_inc(s_logit, 1)
                if n.has(3):
                    guess(3, n, 3)
                if n.has(0):
                    dve.wait_ge(s_out1ps, n(0))
                    dve.wait_ge(s_x1b, n(0))
                    free(dve, s_x2, n(1))
                    dve.tensor_tensor(res1[:, :], ps_a[:, :], x1_b[:, :], ALU.add).then_inc(s_res1, 1)
                    dve.wait_ge(s_res1, n(0))
                    look(1, res1, n, 0)
                    moments(1, n, 0)
                if n.has(1):
                    dve.wait_ge(s_near, n(1))
                    free(dve, s_nmpps, n(2))
                    dve.tensor_tensor(near_adjT[:, :], near[:, :], adjT_in[n.p(1)][:, :], ALU.mult).then_inc(s_nadj, 1)
                if n.has(0):
                    spread(1, n, 0)
                    guess(1, n, 0)
                    newton(1, n, 0, 0, 3)
                if n.has(-1):
                    free(dve, s_dm, n(0))
                    dve.tensor_reduce(deg[:, :], quad(adj_in[n.p(-1)][:, :]), AX.X, ALU.add).then_inc(s_deg, 1)
                if n.has(1):
                    dve.wait_ge(s_nmphi, n(1))
                    free(dve, s_gateps, n(2, 3))
                    dve.tensor_tensor(nmp_lo[:, :], ps_d[:, :], nmp_hi[:, :].bitcast(F32), ALU.subtract).then_inc(s_nmplo, 1)
                if n.has(2):
                    dve.wait_ge(s_lin3ps, n(2))
                    dve.wait_ge(s_scale3, n(2))
                    free(dve, s_lin3d, n(3))
                    dve.tensor_tensor(quad(lin3[:, :]), quad(ps_c[:, :]), per_graph(scale3), ALU.mult).then_inc(s_lin3, 1)
            def sums_and_forms():
                weight_sums()
                affine_forms()

            run(dve, step, {0: sums_and_forms, 1: rest_of_weights})

        @block.gpsimd
        def _(pool):
            def held():
                pool.nop(nofuse=True)

            def newton(i, n, lag):
                v, y_, a = var[i][:, :], rstd[i][:, :], nwt[i][:, :]
                pool.wait_ge(s_guess[i], n(lag))
                for k in range(NEWTON):
                    left = NSTEP[i] - 4 * k
                    if k:
                        pool.wait_ge(s_rstd[i], n(lag, NSTEP[i], left))
                    pool.tensor_tensor(a, y_, y_, ALU.mult).then_inc(s_rstd[i], 1)
                    pool.wait_ge(s_rstd[i], n(lag, NSTEP[i], left - 1))
                    pool.tensor_tensor(a, a, v, ALU.mult).then_inc(s_rstd[i], 1)
                    pool.wait_ge(s_rstd[i], n(lag, NSTEP[i], left - 2))
                    held()
                    pool.tensor_scalar(a, a, -0.5, 1.5, ALU.mult, ALU.add).then_inc(s_rstd[i], 1)
                    pool.wait_ge(s_rstd[i], n(lag, NSTEP[i], left - 3))
                    pool.tensor_tensor(y_, a, y_, ALU.mult).then_inc(s_rstd[i], 1)

            def shifts(i, n, lag):
                pool.wait_ge(s_rstd[i], n(lag, NSTEP[i]))
                pool.tensor_tensor(shift[i][:, :], neg_mean[i][:, :], rstd[i][:, 0:Q], ALU.mult).then_inc(s_shift[i], 1)


            def step(n):
                if n.has(2):
                    halves = conv[:, :].rearrange("p (r q c) -> p r q c", r=2, q=Q)
                    pool.wait_ge(s_z, n(2))
                    pool.wait_ge(s_qs, n(2))
                    pool.tensor_tensor(halves[:, 1], halves[:, 1], conv_q[:, :, 1:PHASE + 1], ALU.add)
                    pool.wait_ge(s_zp, n(2))
                    pool.tensor_tensor(halves[:, 0], halves[:, 0], conv_q[:, :, 0:PHASE], ALU.subtract).then_inc(s_conv, 1)
                if n.has(-1):
                    pool.wait_ge(s_xhi, n(-1))
                    pool.tensor_tensor(xT_lo[:, :], xT_in[n.p(-1)][:, :], xT_hi[:, :].bitcast(F32), ALU.subtract).then_inc(s_xlo, 1)
                if n.has(3):
                    pool.wait_ge(s_relu3, n(3))
                    pool.wait_ge(s_x3, n(3))
                    pool.tensor_tensor(res3[:, :], res3[:, :], x3[:, :], ALU.add).then_inc(s_res3, 1)
                if n.has(1):
                    pool.wait_ge(s_h1hi, n(1))
                    free(pool, s_conv2ps, n(2))
                    inside = slice(PAD // 2, PAD // 2 + PHASE)
                    pool.tensor_tensor(h_lo[:, 0:2, :, inside], phases_q(h1[:, :]), h_hi[:, 0:2, :, inside].bitcast(F32),
                                       ALU.subtract).then_inc(s_h1lo, 1)
                    e = right[:, :, 0:SE]
                    pool.wait_ge(s_emb, n(1))
                    pool.tensor_tensor(s_sq[:, :, :], e, e, ALU.mult).then_inc(s_square, 1)
                if n.has(2):
                    pool.wait_ge(s_gn, n(2))
                    free(pool, s_y, n(3))
                    pool.tensor_tensor(gd[:, :], x2T[n.p(2)][:, :], gn[:, :], ALU.subtract).then_inc(s_gd, 1)
                if n.has(1):
                    pool.tensor_tensor(left[:, :, 0:SE], e, e, ALU.add)
                    pool.wait_ge(s_square, n(1))
                    pool.tensor_tensor(s_sum_t[:, :], s_sq[:, :, 0], s_sq[:, :, 1], ALU.add).then_inc(s_sum, 1)
                if n.has(0):
                    free(pool, s_x1, n(1))
                    shifts(0, n, 0)
                if n.has(1):
                    pool.wait_ge(s_sum, n(1))
                    pool.tensor_tensor(right[:, :, DIST - 1], s_sum_t[:, :], s_sq[:, :, 2], ALU.add).then_inc(s_norm, 1)
                    pool.wait_ge(s_norm, n(1))
                    held()
                    pool.tensor_scalar(left[:, :, SE:SE + 1], right[:, :, DIST - 1:DIST], -1.0, None, ALU.mult).then_inc(s_v, 1)
                    pl, pr = parts(vl[:, :, :]), parts(vr[:, :].rearrange("p (q c) -> p q c", q=Q))
                    pool.wait_ge(s_v, n(1))
                    free(pool, s_vps, n(2))
                    held()
                    pool.tensor_copy(pl[:, :, 0:2, :], twice(left))
                    pool.tensor_copy(pr[:, :, 0:3:2, :], twice(right)).then_inc(s_vhi, 1)
                    pool.wait_ge(s_hshi, n(1))
                    free(pool, s_conv2ps, n(2))
                    inside = slice(PAD // 2, PAD // 2 + PHASE)
                    pool.tensor_tensor(h_lo[:, 2, :, inside], h_sum[:, :].rearrange("p (q c) -> p q c", q=Q),
                                       h_hi[:, 2, :, inside].bitcast(F32), ALU.subtract).then_inc(s_hslo, 1)
                    pl, pr = parts(vl[:, :, :]), parts(vr[:, :].rearrange("p (q c) -> p q c", q=Q))
                    pool.wait_ge(s_vhi, n(1))
                    pool.tensor_tensor(pl[:, :, 2, :], left[:, :, :], pl[:, :, 0, :].bitcast(F32), ALU.subtract)
                    pool.tensor_tensor(pr[:, :, 1, :], right[:, :, :], pr[:, :, 0, :].bitcast(F32), ALU.subtract).then_inc(s_vlo, 1)
                if n.has(0):
                    pool.wait_ge(s_x1, n(0))
                    free(pool, s_res1, n(1))
                    pool.tensor_tensor(quad(x1_b[:, :]), quad(x1[:, :]), row(b1_row), ALU.add).then_inc(s_x1b, 1)
                if n.has(2):
                    pool.wait_ge(s_dmc, n(2))
                    free(pool, s_lin3d, n(3))
                    pool.tensor_tensor(quad(bias3_d[:, :]), row(b3_row), per_graph(dm), ALU.mult).then_inc(s_bias3d, 1)
                    newton(2, n, 2)
                    free(pool, s_x3, n(3))
                    shifts(2, n, 2)
                    pool.wait_ge(s_rstd[2], n(2, NSTEP[2]))
                    pool.wait_ge(s_dmc, n(2))
                    free(pool, s_lin3, n(3))
                    pool.tensor_tensor(scale3[:, :], dm[:, :], rstd[2][:, :], ALU.mult).then_inc(s_scale3, 1)
                if n.has(3):
                    newton(3, n, 3)
                if n.has(0):
                    free(pool, s_x2, n(1))
                    shifts(1, n, 0)
                if n.has(3):
                    free(pool, s_x4, n(4))
                    shifts(3, n, 3)
                if n.has(2):
                    pool.wait_ge(s_lin3, n(2))
                    free(pool, s_out3ps, n(3))
                    pool.wait_ge(s_bias3d, n(2))
                    pool.tensor_tensor(lin3_d[:, :], lin3[:, :], bias3_d[:, :], ALU.add).then_inc(s_lin3d, 1)
            def cleared():
                pool.wait_ge(s_zero, 6)

            run(pool, step, {1: cleared})


def kernel(**inputs):
    import numpy as _np
    import concourse.bacc as _bacc
    from concourse import mybir as _mybir
    from concourse.bass_utils import run_bass_kernel_spmd as _run

    def grouped(a):
        a = _np.asarray(a).reshape(GROUPS, Q, P, P)
        return _np.ascontiguousarray(a.transpose(0, 2, 1, 3)).reshape(GROUPS * P, W)

    def rows(a):
        return _np.ascontiguousarray(_np.asarray(a).T)

    x, adj = _np.asarray(inputs["x"]), _np.asarray(inputs["adj"])
    conv2 = _np.asarray(inputs["L2_gnn_conv2_w"])
    arrays = {
        "x": grouped(x),
        "xT": grouped(x.transpose(0, 2, 1)),
        "adj": grouped(adj),
        "adjT": grouped(adj.transpose(0, 2, 1)),
        "mask": _np.asarray(inputs["nodemask"]).reshape(GROUPS, W),
        "w0": _np.asarray(inputs["L0_gnn_W"]),
        "w1": _np.asarray(inputs["L1_gnn_weight"]),
        "b1": _np.asarray(inputs["L1_gnn_bias"]).reshape(1, P),
        "conv1": rows(_np.asarray(inputs["L2_gnn_conv1_w"]).reshape(P, P)),
        "conv2": _np.ascontiguousarray(conv2.transpose(1, 2, 0)).reshape(P, TAPS * P),
        "bn": _np.ascontiguousarray(_np.stack([_np.asarray(inputs[f"L2_gnn_bn{i}_{v}"])
                                               for i in (1, 2) for v in "gbmv"], axis=1)),
        "wih": rows(inputs["L2_gnn_w_ih"]),
        "whh": rows(inputs["L2_gnn_w_hh"]),
        "bih": rows(_np.asarray(inputs["L2_gnn_b_ih"]).reshape(3, P)),
        "bhh": rows(_np.asarray(inputs["L2_gnn_b_hh"]).reshape(3, P)),
        "wmsg": rows(inputs["L2_gnn_w_msg"]),
        "wse": rows(inputs["L2_gnn_w_se"]),
        "bmsg": _np.asarray(inputs["L2_gnn_b_msg"]).reshape(1, P),
        "bse": _np.asarray(inputs["L2_gnn_b_se"]).reshape(1, SE),
        "w3": rows(inputs["L3_gnn_W"]),
        "b3": _np.asarray(inputs["L3_gnn_b"]).reshape(1, P),
        "eye": _np.eye(P, dtype=_np.float32),
    }
    nc = _bacc.Bacc("TRN2", target_bir_lowering=False, num_devices=1)
    args = [nc.dram_tensor(f"in_{k}", a.shape, _mybir.dt.from_np(a.dtype), kind="ExternalInput").ap()
            for k, a in arrays.items()]
    args.append(nc.dram_tensor("out_0", (GROUPS * P, W), _mybir.dt.float32, kind="ExternalOutput").ap())
    four_gnn_layers(nc, *args)
    r = _run(nc, [{f"in_{k}": a for k, a in arrays.items()}], core_ids=[0])
    out = r.results[0]["out_0"].reshape(GROUPS, P, Q, P)
    return _np.ascontiguousarray(out.transpose(0, 2, 1, 3)).reshape(128, P, P)
```
